# Optimizing a Trainium2 kernel written in Bass

```python
import numpy as np
import jax
import jax.numpy as jnp

def _softmax(x, axis=-1):
    return jax.nn.softmax(x, axis=axis)

def _gelu(x):
    return jax.nn.gelu(x, approximate=True)

def _silu(x):
    return jax.nn.silu(x)

def _sigmoid(x):
    return jax.nn.sigmoid(x)

def _layernorm(x, axis=-1, eps=1e-05):
    m = jnp.mean(x, axis=axis, keepdims=True)
    v = jnp.var(x, axis=axis, keepdims=True)
    return (x - m) / jnp.sqrt(v + eps)

def _scatter_add(tgt, idx, src, axis=0):
    return tgt.at[idx].add(src)

def _segment_sum(src, seg, n):
    return jax.ops.segment_sum(src, seg, n)
kernel_name = 'mk_decoder_postln_d1_seqx_r4_8b5b1a'

def setup_inputs(seed: int=0):
    np.random.seed(seed)
    _w = jnp.asarray

    def _rec_inputs():
        import jax
        import jax.numpy as jnp
        _rk = jax.random.key(seed)
        x = 7.22e-05 + 1 * jax.random.normal(jax.random.fold_in(_rk, 1), (16, 256, 256), jnp.float32)
        _lenS = 256 - jax.random.randint(jax.random.fold_in(_rk, 7), (16,), 0, max(1, 256 // 4) + 1, jnp.int32)
        _lenS2 = 256 - jax.random.randint(jax.random.fold_in(_rk, 8), (16,), 0, max(1, 256 // 4) + 1, jnp.int32)
        _ctx_768P = jax.random.normal(jax.random.fold_in(_rk, 11), (16, 16, 192), jnp.float32)
        _ctx_768c = jax.random.dirichlet(jax.random.fold_in(_rk, 511), 0.3 * jnp.ones((16,), jnp.float32), (16, 256))
        _ctx_768t = jnp.einsum('bsk,bkd->bsd', _ctx_768c, _ctx_768P)
        _ctx_768t = _ctx_768t * jax.lax.rsqrt(jnp.mean(jnp.square(_ctx_768t)) + 1e-12) * 0.953939
        ctx_768 = -0.000191848 + 0.999787 * (_ctx_768t + 0.3 * jax.random.normal(jax.random.fold_in(_rk, 611), (16, 256, 192), jnp.float32))
        return (x, ctx_768)
    x, ctx_768 = _rec_inputs()

    def _L0_attn_setup():
        import jax, jax.numpy as jnp
        import numpy as np
        L, B, D = (512, 8, 256)
        key = jax.random.key(seed)
        ks = jax.random.split(key, 10)
        s = 0.02
        return {'x': jax.random.normal(ks[0], (L, B, D), jnp.float32), 'mu_k': jax.random.uniform(ks[1], (D,), jnp.float32), 'mu_v': jax.random.uniform(ks[2], (D,), jnp.float32), 'mu_r': jax.random.uniform(ks[3], (D,), jnp.float32), 'Wk': jax.random.normal(ks[4], (D, D), jnp.float32) * s, 'Wv': jax.random.normal(ks[5], (D, D), jnp.float32) * s, 'Wr': jax.random.normal(ks[6], (D, D), jnp.float32) * s, 'W_out': jax.random.normal(ks[7], (D, D), jnp.float32) * s, 'w': jax.random.uniform(ks[8], (D,), jnp.float32), 'u': jax.random.uniform(ks[9], (D,), jnp.float32)}
    _L0_attn_all = _L0_attn_setup()
    _L0_attn_in = {k: v for k, v in _L0_attn_all.items() if k in ('mu_k', 'mu_v', 'mu_r', 'Wk', 'Wv', 'Wr', 'W_out', 'w', 'u')}
    del _L0_attn_all

    def _L0_xattn_setup():
        import jax, jax.numpy as jnp
        import numpy as np
        NUM_HEADS = 16
        CLAMP = 10000.0
        key = jax.random.key(seed)
        ks = jax.random.split(key, 8)
        B, Nq, Nkv, Cq, Ckv = (4, 512, 512, 256, 192)
        s_q = 1.0 / np.sqrt(Cq)
        s_kv = 1.0 / np.sqrt(Ckv)
        return {'query': jax.random.normal(ks[0], (B, Nq, Cq), jnp.float32), 'key_value': jax.random.normal(ks[1], (B, Nkv, Ckv), jnp.float32), 'Wq': jax.random.normal(ks[2], (Cq, Cq), jnp.float32) * s_q, 'bq': jnp.zeros((Cq,), jnp.float32), 'Wk': jax.random.normal(ks[3], (Ckv, Cq), jnp.float32) * s_kv, 'bk': jnp.zeros((Cq,), jnp.float32), 'Wv': jax.random.normal(ks[4], (Ckv, Cq), jnp.float32) * s_kv, 'bv': jnp.zeros((Cq,), jnp.float32), 'Wo': jax.random.normal(ks[5], (Cq, Cq), jnp.float32) * s_q, 'bo': jnp.zeros((Cq,), jnp.float32)}
    _L0_xattn_all = _L0_xattn_setup()
    _L0_xattn_in = {k: v for k, v in _L0_xattn_all.items() if k in ('Wq', 'bq', 'Wk', 'bk', 'Wv', 'bv', 'Wo', 'bo')}
    del _L0_xattn_all

    def _L0_ffn_setup():
        import jax, jax.numpy as jnp
        import numpy as np
        B, S, H = (2, 256, 256)
        E, F = (16, 128)
        G, TOPK_G, TOPK = (4, 2, 4)
        N_SHARED = 2
        ROUTE_SCALE = 1.0
        FS = N_SHARED * F

        def _gate(x, w_gate):
            T = x.shape[0]
            scores = jax.nn.sigmoid(x @ w_gate.T)
            sv = scores.reshape(T, G, E // G)
            group_scores = jax.lax.top_k(sv, 2)[0].sum(-1)
            top_groups = jax.lax.top_k(group_scores, TOPK_G)[1]
            allowed = jnp.zeros((T, G), dtype=bool).at[jnp.arange(T)[:, None], top_groups].set(True)
            masked = jnp.where(allowed[:, :, None], sv, -jnp.inf).reshape(T, E)
            _, idx = jax.lax.top_k(masked, TOPK)
            w = jnp.take_along_axis(scores, idx, axis=1)
            w = w / (w.sum(-1, keepdims=True) + 1e-06) * ROUTE_SCALE
            return (w, idx)

        def _swiglu(x, w1, w3, w2):
            return jax.nn.silu(x @ w1.T) * (x @ w3.T) @ w2.T
        key = jax.random.key(seed)
        ks = jax.random.split(key, 8)
        scale = 0.02
        return {'hidden_states': jax.random.normal(ks[0], (B, S, H), dtype=jnp.float32), 'w_gate': jax.random.normal(ks[1], (E, H), dtype=jnp.float32) * scale, 'w1_e': jax.random.normal(ks[2], (E, F, H), dtype=jnp.float32) * scale, 'w3_e': jax.random.normal(ks[3], (E, F, H), dtype=jnp.float32) * scale, 'w2_e': jax.random.normal(ks[4], (E, H, F), dtype=jnp.float32) * scale, 'w1_s': jax.random.normal(ks[5], (FS, H), dtype=jnp.float32) * scale, 'w3_s': jax.random.normal(ks[6], (FS, H), dtype=jnp.float32) * scale, 'w2_s': jax.random.normal(ks[7], (H, FS), dtype=jnp.float32) * scale}
    _L0_ffn_all = _L0_ffn_setup()
    _L0_ffn_in = {k: v for k, v in _L0_ffn_all.items() if k in ('w_gate', 'w1_e', 'w3_e', 'w2_e', 'w1_s', 'w3_s', 'w2_s')}
    del _L0_ffn_all
    return {'x': x, 'ctx_768': ctx_768, 'L0_attn_mu_k': _L0_attn_in['mu_k'], 'L0_attn_mu_v': _L0_attn_in['mu_v'], 'L0_attn_mu_r': _L0_attn_in['mu_r'], 'L0_attn_Wk': _L0_attn_in['Wk'], 'L0_attn_Wv': _L0_attn_in['Wv'], 'L0_attn_Wr': _L0_attn_in['Wr'], 'L0_attn_W_out': _L0_attn_in['W_out'], 'L0_attn_w': _L0_attn_in['w'], 'L0_attn_u': _L0_attn_in['u'], 'L0_xattn_Wq': _L0_xattn_in['Wq'], 'L0_xattn_bq': _L0_xattn_in['bq'], 'L0_xattn_Wk': _L0_xattn_in['Wk'], 'L0_xattn_bk': _L0_xattn_in['bk'], 'L0_xattn_Wv': _L0_xattn_in['Wv'], 'L0_xattn_bv': _L0_xattn_in['bv'], 'L0_xattn_Wo': _L0_xattn_in['Wo'], 'L0_xattn_bo': _L0_xattn_in['bo'], 'L0_ffn_w_gate': _L0_ffn_in['w_gate'], 'L0_ffn_w1_e': _L0_ffn_in['w1_e'], 'L0_ffn_w3_e': _L0_ffn_in['w3_e'], 'L0_ffn_w2_e': _L0_ffn_in['w2_e'], 'L0_ffn_w1_s': _L0_ffn_in['w1_s'], 'L0_ffn_w3_s': _L0_ffn_in['w3_s'], 'L0_ffn_w2_s': _L0_ffn_in['w2_s']}

def reference(x, ctx_768, L0_attn_mu_k, L0_attn_mu_v, L0_attn_mu_r, L0_attn_Wk, L0_attn_Wv, L0_attn_Wr, L0_attn_W_out, L0_attn_w, L0_attn_u, L0_xattn_Wq, L0_xattn_bq, L0_xattn_Wk, L0_xattn_bk, L0_xattn_Wv, L0_xattn_bv, L0_xattn_Wo, L0_xattn_bo, L0_ffn_w_gate, L0_ffn_w1_e, L0_ffn_w3_e, L0_ffn_w2_e, L0_ffn_w1_s, L0_ffn_w3_s, L0_ffn_w2_s):
    import jax
    import jax.numpy as jnp

    def _L0_attn_ref(x, mu_k, mu_v, mu_r, Wk, Wv, Wr, W_out, w, u):
        import jax, jax.numpy as jnp
        import numpy as np
        L, B, D = (512, 8, 256)
        Lx = x.shape[0]
        x_prev = jnp.concatenate([jnp.zeros_like(x[:1]), x[:-1]], axis=0)
        k = (mu_k * x + (1.0 - mu_k) * x_prev) @ Wk.T
        v = (mu_v * x + (1.0 - mu_v) * x_prev) @ Wv.T
        r = (mu_r * x + (1.0 - mu_r) * x_prev) @ Wr.T
        w_neg = -jnp.exp(w)
        exp_w = jnp.exp(w_neg)
        t = jnp.arange(Lx, dtype=x.dtype)
        ewp = jnp.exp(w_neg[None, :] * t[:, None])
        exp_k = jnp.exp(k)
        exp_k_v = exp_k * v
        n = 2 * Lx
        f_ewp = jnp.fft.rfft(ewp, n=n, axis=0)[:, None, :]
        f_ek = jnp.fft.rfft(exp_k, n=n, axis=0)
        f_ekv = jnp.fft.rfft(exp_k_v, n=n, axis=0)
        conv_ek = jnp.fft.irfft(f_ewp * f_ek, axis=0)[:Lx]
        conv_ekv = jnp.fft.irfft(f_ewp * f_ekv, axis=0)[:Lx]
        denominator = conv_ek
        numerator = conv_ekv
        exp_u = jnp.exp(u)
        denominator_out = (denominator - exp_k) / exp_w + exp_k * exp_u
        numerator_out = (numerator - exp_k_v) / exp_w + exp_k_v * exp_u
        return jax.nn.sigmoid(r) * numerator_out / denominator_out @ W_out.T

    def _L0_xattn_ref(query, key_value, Wq, bq, Wk, bk, Wv, bv, Wo, bo):
        import jax, jax.numpy as jnp
        import numpy as np
        NUM_HEADS = 16
        CLAMP = 10000.0
        B, Nq, Cq = query.shape
        Nkv = key_value.shape[1]
        H = NUM_HEADS
        D = Cq // H
        scale = D ** (-0.5)
        q = (query @ Wq + bq).reshape(B, Nq, H, D).transpose(0, 2, 1, 3)
        k = (key_value @ Wk + bk).reshape(B, Nkv, H, D).transpose(0, 2, 1, 3)
        v = (key_value @ Wv + bv).reshape(B, Nkv, H, D).transpose(0, 2, 1, 3)
        attn = jnp.einsum('bhqd,bhkd->bhqk', q, k) * scale
        attn = jnp.clip(attn, -CLAMP, CLAMP)
        attn = jax.nn.softmax(attn, axis=-1)
        attn = jnp.where(jnp.any(jnp.isnan(attn)), jnp.asarray(1.0 / Nkv, attn.dtype), attn)
        x = jnp.einsum('bhqk,bhkd->bqhd', attn, v).reshape(B, Nq, Cq)
        return x @ Wo + bo

    def _L0_ffn_ref(hidden_states, w_gate, w1_e, w3_e, w2_e, w1_s, w3_s, w2_s):
        import jax, jax.numpy as jnp
        import numpy as np
        B, S, H = (2, 256, 256)
        E, F = (16, 128)
        G, TOPK_G, TOPK = (4, 2, 4)
        N_SHARED = 2
        ROUTE_SCALE = 1.0
        FS = N_SHARED * F

        def _gate(x, w_gate):
            T = x.shape[0]
            scores = jax.nn.sigmoid(x @ w_gate.T)
            sv = scores.reshape(T, G, E // G)
            group_scores = jax.lax.top_k(sv, 2)[0].sum(-1)
            top_groups = jax.lax.top_k(group_scores, TOPK_G)[1]
            allowed = jnp.zeros((T, G), dtype=bool).at[jnp.arange(T)[:, None], top_groups].set(True)
            masked = jnp.where(allowed[:, :, None], sv, -jnp.inf).reshape(T, E)
            _, idx = jax.lax.top_k(masked, TOPK)
            w = jnp.take_along_axis(scores, idx, axis=1)
            w = w / (w.sum(-1, keepdims=True) + 1e-06) * ROUTE_SCALE
            return (w, idx)

        def _swiglu(x, w1, w3, w2):
            return jax.nn.silu(x @ w1.T) * (x @ w3.T) @ w2.T
        shape = hidden_states.shape
        x = hidden_states.reshape(-1, H)
        weights, idx = _gate(x, w_gate)
        combine = (jax.nn.one_hot(idx, E, dtype=x.dtype) * weights[..., None]).sum(1)
        g = jax.nn.silu(jnp.einsum('th,efh->tef', x, w1_e))
        u = jnp.einsum('th,efh->tef', x, w3_e)
        routed = jnp.einsum('tef,ehf,te->th', g * u, w2_e, combine)
        shared = _swiglu(x, w1_s, w3_s, w2_s)
        return (routed + shared).reshape(shape)
    x = _layernorm(x + _L0_attn_ref(x, L0_attn_mu_k, L0_attn_mu_v, L0_attn_mu_r, L0_attn_Wk, L0_attn_Wv, L0_attn_Wr, L0_attn_W_out, L0_attn_w, L0_attn_u), axis=-1)
    x = _layernorm(x + _L0_xattn_ref(x, ctx_768, L0_xattn_Wq, L0_xattn_bq, L0_xattn_Wk, L0_xattn_bk, L0_xattn_Wv, L0_xattn_bv, L0_xattn_Wo, L0_xattn_bo), axis=-1)
    x = _layernorm(x + _L0_ffn_ref(x, L0_ffn_w_gate, L0_ffn_w1_e, L0_ffn_w3_e, L0_ffn_w2_e, L0_ffn_w1_s, L0_ffn_w3_s, L0_ffn_w2_s), axis=-1)
    return x

_drawn_inputs = setup_inputs


def setup_inputs(seed=0):
    import zlib

    import numpy as np

    out = dict(_drawn_inputs(seed))
    spreads = {'L0_xattn_bq': (0.0, 0.1),
     'L0_xattn_bk': (0.0, 0.1),
     'L0_xattn_bv': (0.0, 0.1),
     'L0_xattn_bo': (0.0, 0.1)}
    factors = {}
    for name, (base, spread) in spreads.items():
        noise = np.random.default_rng([zlib.crc32(name.encode()), seed]).standard_normal(out[name].shape)
        drawn = base * np.exp(spread * noise) if base else spread * noise
        out[name] = jnp.asarray(drawn.astype(out[name].dtype))
    for name, factor in factors.items():
        out[name] = (out[name] * factor).astype(out[name].dtype)
    return out
```

```python
from contextlib import ExitStack

import numpy as np

import concourse.bass as bass
from concourse import mybir

F32 = mybir.dt.float32
ACT = mybir.ActivationFunctionType
ALU = mybir.AluOpType
AX = mybir.AxisListType

P = 128
L, TOK, D = 16, 256, 256
CKV = 192
CP = CKV // 2
NT = TOK // P
ND = D // P
HEADS, HD = 16, 16
HG = P // HD
E, F = 16, 128
GROUPS, TOPG, TOPK = 4, 2, 4
EG = E // GROUPS
PAIRS = E // 2 + 1
SCALE = float(HD) ** -0.5
CLAMP = 10000.0
EPS = 1e-5
VBLOCK = HG * (P + HD)


class Step:

    def __init__(self, i, off):
        self.i, self.off = i, off
        self.l = 2 * i + off
        self.half = i + off // 2
        self.par = off % 2

    def plus(self, k):
        return Step(self.i, self.off + k)


class Event:

    def __init__(self, sem, per):
        self.sem, self.per = sem, per

    def at(self, step, k=None):
        return step.l * self.per + (self.per if k is None else k)


def first(step):
    return isinstance(step.l, int) and step.l == 0


VECS = ["mu_k", "mu_v", "mu_r", "w", "u", "bq", "bk"]


def decoder_layer(nc, x, xT, ctxT, vecs, rows, wproj, wctx, w1, w3, w2, wg, ident, sel, parity, below, out):
    with ExitStack() as ctx:
        def sb(name, shape, dt=F32):
            return ctx.enter_context(nc.sbuf_tensor(name, shape, dt))

        def bank(name):
            return ctx.enter_context(nc.psum_tensor(name, [P, 512], F32))

        def sem(name):
            return ctx.enter_context(nc.semaphore(name))

        def event(name, per=1):
            return Event(sem(name), per)

        Wp = sb("Wp", [P, 6, ND, D])
        WK, WV, WR, WOUT, WQ, WO = range(6)
        Wc = sb("Wc", [CP, 2, 2, D])
        W1 = sb("W1", [P, ND, 2 * PAIRS * F])
        W3 = sb("W3", [P, ND, 2 * PAIRS * F])
        W2 = sb("W2", [P, 2 * PAIRS, D])
        Wg = sb("Wg", [P, ND, E])
        idn = sb("idn", [P, P])
        selh = sb("selh", [HEADS, ND, P])
        par_mask = sb("par_mask", [P, 2])
        lower = sb("lower", [P, E, E])
        vec = sb("vec", [P, len(VECS), ND])
        bv_row = sb("bv_row", [P, D])
        bo_row = sb("bo_row", [P, D])
        decay = sb("decay", [P, ND])
        ew = sb("ew", [P, ND])
        eu = sb("eu", [P, ND])
        qscale = sb("qscale", [P, 2])
        qbias = sb("qbias", [P, 2, ND])
        mhalf = sb("mhalf", [P, NT])

        xTs = sb("xTs", [P, 2, ND, TOK])
        xs = sb("xs", [P, 2, NT, D])
        cT = sb("cT", [CP, 2, 2, TOK])
        dx = sb("dx", [P, ND, TOK])
        mix = sb("mix", [P, 3, ND, TOK])
        ek = sb("ek", [P, ND, TOK])
        ekv = sb("ekv", [P, ND, TOK])
        thr = sb("thr", [P, ND, TOK])
        den = sb("den", [P, ND, TOK])
        num = sb("num", [P, ND, TOK])
        Sd = sb("Sd", [P, ND, TOK])
        Sn = sb("Sn", [P, ND, TOK])
        wkv = sb("wkv", [P, ND, TOK])
        z1 = sb("z1", [P, NT, D])
        x1 = sb("x1", [P, NT, D])
        x1T = sb("x1T", [P, ND, TOK])
        x1b = sb("x1b", [P, 2, NT, D])
        QT = sb("QT", [P, 2, 2, ND, TOK])
        KT = sb("KT", [P, 2, ND, TOK])
        Vs = sb("Vs", [P, NT, D])
        Vz = sb("Vz", [P, NT, ND * VBLOCK])

        Sc = sb("Sc", [P, 2, NT, TOK])
        nmx = sb("nmx", [P, HEADS, NT])
        Pr = sb("Pr", [P, 2, NT, TOK])
        rs = sb("rs", [P, NT, HEADS])
        rr = sb("rr", [P, NT, HEADS])
        PT = sb("PT", [P, 2, NT, TOK])
        rT = sb("rT", [HEADS, TOK])
        Rb = sb("Rb", [P, ND, TOK])
        aoT = sb("aoT", [P, ND, TOK])
        z2 = sb("z2", [P, NT, D])
        gth = sb("gth", [P, NT * E])
        sc = sb("sc", [P, NT, E])
        pair = sb("pair", [P, NT * GROUPS, 6])
        gsum = sb("gsum", [P, NT, GROUPS])
        ggt = sb("ggt", [P, NT, GROUPS, GROUPS])
        geq = sb("geq", [P, NT, GROUPS, GROUPS])
        grank = sb("grank", [P, NT, GROUPS])
        gok = sb("gok", [P, NT, GROUPS])
        msk = sb("msk", [P, NT, E])
        egt = sb("egt", [P, NT, E, E])
        eeq = sb("eeq", [P, NT, E, E])
        erank = sb("erank", [P, NT, E])
        wsel = sb("wsel", [P, NT, E])
        wsum = sb("wsum", [P, NT])
        wrec = sb("wrec", [P, NT])
        x2 = sb("x2", [P, 2, NT, D])
        x2T = sb("x2T", [P, 2, ND, TOK])
        comb = sb("comb", [P, 2, NT, E])

        tg = sb("tg", [P, 2, TOK])
        t1 = sb("t1", [P, 2, TOK])
        hid = sb("hid", [P, 2, 2, TOK])
        acc = sb("acc", [P, NT, D])
        yo = sb("yo", [P, 2, NT, D])

        st = sb("st", [P, 3, NT, 6])
        mv = sb("mv", [P, 3, NT, 2])
        vpe = sb("vpe", [P, 3, NT])
        rstd = sb("rstd", [P, 3, NT])

        bG, bU, bY0, bY1, bS, bT, bO, bM = (bank(n) for n in ("bG", "bU", "bY0", "bY1", "bS", "bT", "bO", "bM"))
        bY = [bY0, bY1]

        def cols(b, n=2):
            return b[:, :].rearrange("p (n c) -> p n c", n=n)

        s_att = sem("s_att")
        s_ffn = sem("s_ffn")
        s_const = sem("s_const")
        s_zero = sem("s_zero")
        s_ew = sem("s_ew")
        s_decay = sem("s_decay")
        s_qs = sem("s_qs")
        s_qb = sem("s_qb")
        s_in = [sem("s_in0"), sem("s_in1")]
        s_out = [sem("s_out0"), sem("s_out1")]
        d_dx = event("d_dx")
        d_mix = event("d_mix", 3)
        p_kvr = event("p_kvr", 3)
        a_ek = event("a_ek")
        d_ekv = event("d_ekv")
        a_thr = event("a_thr")
        d_den = event("d_den", 2)
        d_state = event("d_state", 2)
        d_wkv = event("d_wkv", 2)
        p_wout = event("p_wout")
        d_z1 = event("d_z1")
        d_x1 = event("d_x1")
        g_x1b = event("g_x1b")
        p_x1T = event("p_x1T")
        a_x1T = event("a_x1T")
        p_q = event("p_q")
        a_q = event("a_q")
        p_k = event("p_k")
        a_k = event("a_k")
        p_v = event("p_v")
        a_v = event("a_v")
        g_v = event("g_v")
        d_st = [event(f"d_st{n}") for n in range(3)]
        d_mv = [event(f"d_mv{n}") for n in range(3)]
        d_vpe = [event(f"d_vpe{n}") for n in range(3)]
        g_rstd = [event(f"g_rstd{n}") for n in range(3)]
        p_s = event("p_s", HEADS)
        d_clip = event("d_clip", HEADS)
        d_max = event("d_max", HEADS)
        a_exp = event("a_exp", HEADS)
        p_t = event("p_t", HEADS)
        a_pt = event("a_pt", HEADS)
        p_av = event("p_av", HEADS)
        d_rr = event("d_rr")
        p_rT = event("p_rT")
        a_rT = event("a_rT")
        p_R = event("p_R")
        a_R = event("a_R")
        d_ao = event("d_ao")
        p_wo = event("p_wo")
        d_z2 = event("d_z2")
        d_x2 = event("d_x2")
        p_x2T = event("p_x2T")
        a_x2T = event("a_x2T")
        p_gate = event("p_gate")
        a_gate = event("a_gate")
        d_gate = event("d_gate", 13)
        p_g = event("p_g", PAIRS)
        p_u = event("p_u", PAIRS)
        a_tg = event("a_tg", PAIRS)
        d_t1 = event("d_t1", PAIRS)
        d_h = event("d_h", PAIRS)
        p_y = event("p_y", 2 * PAIRS - 1)
        d_acc = event("d_acc", 2 * PAIRS - 1)
        d_yo = event("d_yo")

        block = ctx.enter_context(nc.Block())

        def bodies(eng, body):
            body(Step(0, -1), True, False, False)
            body(Step(0, 0), True, True, False)
            body(Step(0, 1), True, True, True)
            body(Step(0, 2), True, True, True)
            with eng.Fori(1, (L - 2) // 2) as i:
                body(Step(i, 1), True, True, True)
                body(Step(i, 2), True, True, True)
            body(Step(L // 2, -1), False, True, True)
            body(Step(L // 2, 0), False, False, True)

        @block.sync
        def _(sp):
            def load(step, first=False):
                p = step.par
                sp.dma_start(xTs[:, p], xT[bass.ds(step.l, 1)].rearrange("a (j p) t -> p (a j) t", p=P)).then_inc(s_in[p], 16)
                sp.dma_start(cT[:, p], ctxT[bass.ds(step.l, 1)].rearrange("a (j p) t -> p (a j) t", p=CP)).then_inc(s_in[p], 16)
                sp.dma_start(xs[:, p], x[bass.ds(step.l, 1)].rearrange("a (t p) d -> p (a t) d", p=P)).then_inc(s_in[p], 16)

            sp.dma_start(vec[:, :, :], vecs).then_inc(s_const, 16)
            sp.dma_start(par_mask[:, :], parity).then_inc(s_const, 16)
            load(Step(0, 0))
            sp.dma_start(Wp[:, :, :, :], wproj.rearrange("w (j p) d -> p w j d", p=P)).then_inc(s_att, 16)
            sp.dma_start(Wc[:, :, :, :], wctx.rearrange("w (j p) d -> p w j d", p=CP)).then_inc(s_att, 16)
            sp.dma_start(idn[:, :], ident).then_inc(s_const, 16)
            sp.dma_start(bv_row[:, :], rows[0]).then_inc(s_const, 16)
            sp.dma_start(bo_row[:, :], rows[1]).then_inc(s_const, 16)
            sp.dma_start(selh[:, :, :], sel).then_inc(s_const, 16)
            sp.dma_start(lower[:, :, :], below).then_inc(s_const, 16)
            sp.dma_start(Wg[:, :, :], wg.rearrange("(j p) e -> p j e", p=P)).then_inc(s_const, 16)
            sp.dma_start(W1[:, :, :], w1.rearrange("(j p) f -> p j f", p=P)).then_inc(s_ffn, 16)
            sp.dma_start(W3[:, :, :], w3.rearrange("(j p) f -> p j f", p=P)).then_inc(s_ffn, 16)
            sp.dma_start(W2[:, :, :], w2.rearrange("c p h -> p c h")).then_inc(s_ffn, 16)

            def body(s, A, B, C):
                a, c = s.plus(1), s.plus(-1)
                if A and not (isinstance(a.l, int) and a.l == L - 1):
                    sp.wait_ge(d_mix.sem, d_mix.at(a))
                    load(a.plus(1))
                if C:
                    sp.wait_ge(d_yo.sem, d_yo.at(c))
                    sp.dma_start(out[bass.ds(c.l, 1)].rearrange("a (t p) d -> p (a t) d", p=P), yo[:, c.par]).then_inc(s_out[c.par], 16)

            body(Step(0, -1), True, False, False)
            sp.wait_ge(s_zero, 1)
            body(Step(0, 0), True, True, False)
            body(Step(0, 1), True, True, True)
            body(Step(0, 2), True, True, True)
            with sp.Fori(1, (L - 4) // 2) as i:
                body(Step(i, 1), True, True, True)
                body(Step(i, 2), True, True, True)
            body(Step((L - 4) // 2, 1), True, True, True)
            body(Step((L - 4) // 2, 2), True, True, True)
            body(Step(L // 2, -1), False, True, True)
            body(Step(L // 2, 0), False, False, True)
            for p in range(2):
                sp.wait_ge(s_out[p], 16 * L // 2)

        @block.tensor
        def _(pe):
            mm = pe.matmul

            def proj(dst, w, src, n):
                for m in range(ND):
                    for j in range(n):
                        last = mm(dst[:, m, :], w[:, j, m * P:(m + 1) * P], src[:, j, :], start=(j == 0), stop=(j == n - 1))
                return last

            def token_proj(dst, w, src, n):
                for t in range(NT):
                    for j in range(n):
                        last = mm(dst[:, t, :], src[:, j, t * P:(t + 1) * P], w[:, j, :], start=(j == 0), stop=(j == n - 1))
                return last

            def turn(dst, src):
                for j in range(ND):
                    for t in range(NT):
                        last = pe.transpose(dst[:, j, t * P:(t + 1) * P], src[:, t, j * P:(j + 1) * P], idn[:, :])
                return last

            M = cols(bM)

            def a_chunk(s, n):
                if n == 0:
                    if first(s):
                        pe.wait_ge(s_att, 32)
                    pe.wait_ge(d_mix.sem, d_mix.at(s, 1))
                    proj(M, Wp[:, WK], mix[:, 0], ND).then_inc(p_kvr.sem, 1)
                elif n == 1:
                    pe.wait_ge(d_mix.sem, d_mix.at(s, 2))
                    pe.wait_ge(a_ek.sem, a_ek.at(s))
                    proj(M, Wp[:, WV], mix[:, 1], ND).then_inc(p_kvr.sem, 1)
                elif n == 2:
                    pe.wait_ge(d_mix.sem, d_mix.at(s, 3))
                    pe.wait_ge(d_ekv.sem, d_ekv.at(s))
                    proj(M, Wp[:, WR], mix[:, 2], ND).then_inc(p_kvr.sem, 1)
                elif n == 3:
                    pe.wait_ge(a_thr.sem, a_thr.at(s))
                    proj(M, Wc[:, 0], cT[:, s.par], 2).then_inc(p_k.sem, 1)
                elif n == 4:
                    pe.wait_ge(a_k.sem, a_k.at(s))
                    token_proj(M, Wc[:, 1], cT[:, s.par], 2).then_inc(p_v.sem, 1)
                elif n == 5:
                    pe.wait_ge(a_v.sem, a_v.at(s))
                    pe.wait_ge(d_wkv.sem, d_wkv.at(s))
                    token_proj(M, Wp[:, WOUT], wkv, ND).then_inc(p_wout.sem, 1)
                elif n == 6:
                    pe.wait_ge(d_z1.sem, d_z1.at(s))
                    pe.wait_ge(d_x1.sem, d_x1.at(s))
                    turn(M, x1).then_inc(p_x1T.sem, 1)
                elif n == 7:
                    pe.wait_ge(a_x1T.sem, a_x1T.at(s))
                    proj(M, Wp[:, WQ], x1T, ND).then_inc(p_q.sem, 1)

            def scores(s, h):
                g, m = divmod(h, HG)
                r = 32 * (m // 2)
                if h == 0:
                    pe.wait_ge(a_q.sem, a_q.at(s))
                    pe.wait_ge(a_k.sem, a_k.at(s))
                    pe.wait_ge(a_v.sem, a_v.at(s))
                    if not first(s):
                        pe.wait_ge(d_clip.sem, d_clip.at(s.plus(-1)))
                else:
                    pe.wait_ge(d_clip.sem, d_clip.at(s, h))
                S = cols(bS)
                for t in range(NT):
                    last = mm(S[:, t, :], QT[r:r + 32, s.par, m % 2, g, t * P:(t + 1) * P], KT[r:r + 32, s.par, g, :], start=True, stop=True)
                last.then_inc(p_s.sem, 1)

            def turn_probs(s, h):
                pe.wait_ge(a_exp.sem, a_exp.at(s, h + 1))
                if h:
                    pe.wait_ge(a_pt.sem, a_pt.at(s, h))
                turn(cols(bT), Pr[:, h % 2]).then_inc(p_t.sem, 1)

            def values(s, h):
                g, m = divmod(h, HG)
                pe.wait_ge(a_pt.sem, a_pt.at(s, h + 1))
                if h == 0:
                    pe.wait_ge(g_v.sem, g_v.at(s))
                if h == 0 and not first(s):
                    pe.wait_ge(d_ao.sem, d_ao.at(s.plus(-1)))
                O = cols(bO)
                c = g * VBLOCK + m * P
                for k in range(NT):
                    last = mm(O[:, g, :], Vz[:, k, c:c + P], PT[:, h % 2, k, :], start=(m == 0 and k == 0), stop=(m == HG - 1 and k == NT - 1))
                last.then_inc(p_av.sem, 1)

            def b_tail(s, n, a):
                if n == 0:
                    pe.wait_ge(d_rr.sem, d_rr.at(s))
                    if a is not None:
                        pe.wait_ge(a_q.sem, a_q.at(a))
                    for t in range(NT):
                        last = pe.transpose(bM[0:HEADS, t * P:(t + 1) * P], rr[:, t, :], idn[:, :])
                    last.then_inc(p_rT.sem, 1)
                elif n == 1:
                    pe.wait_ge(a_rT.sem, a_rT.at(s))
                    for g in range(ND):
                        last = mm(M[:, g, :], selh[:, g, :], rT[:, :], start=True, stop=True)
                    last.then_inc(p_R.sem, 1)
                elif n == 2:
                    pe.wait_ge(d_ao.sem, d_ao.at(s))
                    token_proj(M, Wp[:, WO], aoT, ND).then_inc(p_wo.sem, 1)
                elif n == 3:
                    pe.wait_ge(d_x2.sem, d_x2.at(s))
                    turn(M, x2[:, s.par]).then_inc(p_x2T.sem, 1)
                elif n == 4:
                    pe.wait_ge(a_x2T.sem, a_x2T.at(s))
                    for t in range(NT):
                        for j in range(ND):
                            last = mm(bM[:, t * E:(t + 1) * E], x2T[:, s.par, j, t * P:(t + 1) * P], Wg[:, j, :], start=(j == 0), stop=(j == ND - 1))
                    last.then_inc(p_gate.sem, 1)

            def gate_up(s, k, w, b, done, read):
                if k == 0:
                    pe.wait_ge(a_x2T.sem, a_x2T.at(s))
                    if not first(s):
                        pe.wait_ge(read.sem, read.at(s.plus(-1)))
                else:
                    pe.wait_ge(read.sem, read.at(s, k))
                dst = cols(b)
                for i in range(2):
                    c = (2 * k + i) * F
                    for j in range(ND):
                        last = mm(dst[:, i, :], w[:, j, c:c + F], x2T[:, s.par, j, :], start=(j == 0), stop=(j == ND - 1))
                last.then_inc(done.sem, 1)

            def down(s, k, i):
                pe.wait_ge(d_h.sem, d_h.at(s, k + 1))
                if k == 0:
                    if not first(s):
                        pe.wait_ge(d_acc.sem, d_acc.at(s.plus(-1)))
                elif k == 1 and i == 0:
                    pe.wait_ge(d_acc.sem, d_acc.at(s, 1))
                elif k > 1:
                    pe.wait_ge(d_acc.sem, d_acc.at(s, 2 * (k - 1) + i))
                dst = cols(bY[i])
                for t in range(NT):
                    for c in ((0, 1) if k == 0 else (i,)):
                        last = mm(dst[:, t, :], hid[:, k % 2, c, t * P:(t + 1) * P], W2[:, 2 * k + c, :],
                                  start=(k > 0 or c == 0), stop=(k > 0 or c == 1))
                last.then_inc(p_y.sem, 1)

            def body(s, A, B, C):
                a, c = s.plus(1), s.plus(-1)
                for k in range(PAIRS + 1):
                    h = 2 * k
                    heads = B and h < HEADS
                    if heads:
                        scores(s, h)
                    if C and k < PAIRS:
                        gate_up(c, k, W1, bG, p_g, d_t1)
                    if B and 0 < h <= HEADS:
                        turn_probs(s, h - 1)
                    if C and k < PAIRS:
                        gate_up(c, k, W3, bU, p_u, d_h)
                    if B and 0 < h <= HEADS:
                        values(s, h - 1)
                    if heads:
                        scores(s, h + 1)
                    if C and k:
                        down(c, k - 1, 0)
                    if heads:
                        turn_probs(s, h)
                    if C and k > 1:
                        down(c, k - 1, 1)
                    if heads:
                        values(s, h)
                    if A and k < 8:
                        a_chunk(a, k)
                if B:
                    for n in range(5):
                        b_tail(s, n, a if A else None)

            pe.wait_ge(s_const, 16 * 8)
            pe.wait_ge(s_zero, 1)
            body(Step(0, -1), True, False, False)
            body(Step(0, 0), True, True, False)
            pe.wait_ge(s_ffn, 48)
            body(Step(0, 1), True, True, True)
            body(Step(0, 2), True, True, True)
            with pe.Fori(1, (L - 2) // 2) as i:
                body(Step(i, 1), True, True, True)
                body(Step(i, 2), True, True, True)
            body(Step(L // 2, -1), False, True, True)
            body(Step(L // 2, 0), False, False, True)

        @block.scalar
        def _(act):
            fn = act.activation
            M = bM[:, :]

            def flat(t):
                return t.rearrange("p a b -> p (a b)")

            act.wait_ge(s_const, 16 * 8)
            fn(ew[:, :], vec[:, 3, :], ACT.Exp).then_inc(s_ew, 1)
            fn(eu[:, :], vec[:, 4, :], ACT.Exp)
            act.wait_ge(s_ew, 1)
            fn(decay[:, :], ew[:, :], ACT.Exp, scale=-1.0).then_inc(s_decay, 1)
            act.wait_ge(s_qb, 1)

            def a_chunk(s, n):
                if n == 0:
                    act.wait_ge(p_kvr.sem, p_kvr.at(s, 1))
                    fn(flat(ek[:, :, :]), M, ACT.Exp).then_inc(a_ek.sem, 1)
                elif n == 2:
                    act.wait_ge(p_kvr.sem, p_kvr.at(s, 3))
                    fn(flat(thr[:, :, :]), M, ACT.Tanh, scale=0.5).then_inc(a_thr.sem, 1)
                elif n == 3:
                    act.wait_ge(p_k.sem, p_k.at(s))
                    for j in range(ND):
                        last = fn(KT[:, s.par, j, :], cols(bM)[:, j, :], ACT.Identity, bias=vec[:, 6, j:j + 1])
                    last.then_inc(a_k.sem, 1)
                elif n == 4:
                    act.wait_ge(p_v.sem, p_v.at(s))
                    if not first(s):
                        act.wait_ge(g_v.sem, g_v.at(s.plus(-1)))
                    fn(flat(Vs[:, :, :]), M, ACT.Copy).then_inc(a_v.sem, 1)
                elif n == 6:
                    act.wait_ge(p_x1T.sem, p_x1T.at(s))
                    fn(flat(x1T[:, :, :]), M, ACT.Copy).then_inc(a_x1T.sem, 1)
                elif n == 7:
                    act.wait_ge(p_q.sem, p_q.at(s))
                    for hp in range(2):
                        for j in range(ND):
                            last = fn(QT[:, s.par, hp, j, :], cols(bM)[:, j, :], ACT.Identity,
                                      bias=qbias[:, hp, j:j + 1], scale=qscale[:, hp:hp + 1])
                    last.then_inc(a_q.sem, 1)

            def exps(s, h):
                act.wait_ge(d_max.sem, d_max.at(s, h + 1))
                if h >= 2:
                    act.wait_ge(p_t.sem, p_t.at(s, h - 1))
                for t in range(NT):
                    last = fn(Pr[:, h % 2, t, :], Sc[:, h % 2, t, :], ACT.Exp, bias=nmx[:, h, t:t + 1], accum_out=rs[:, t, h:h + 1])
                last.then_inc(a_exp.sem, 1)

            def copy_probs(s, h):
                act.wait_ge(p_t.sem, p_t.at(s, h + 1))
                if h >= 2:
                    act.wait_ge(p_av.sem, p_av.at(s, h - 1))
                fn(flat(PT[:, h % 2]), bT[:, :], ACT.Copy).then_inc(a_pt.sem, 1)

            def b_tail(s, n):
                if n == 0:
                    act.wait_ge(p_rT.sem, p_rT.at(s))
                    fn(rT[:, :], bM[0:HEADS, 0:TOK], ACT.Copy).then_inc(a_rT.sem, 1)
                elif n == 1:
                    act.wait_ge(p_R.sem, p_R.at(s))
                    fn(flat(Rb[:, :, :]), M, ACT.Copy).then_inc(a_R.sem, 1)
                elif n == 3:
                    act.wait_ge(p_x2T.sem, p_x2T.at(s))
                    fn(flat(x2T[:, s.par]), M, ACT.Copy).then_inc(a_x2T.sem, 1)
                elif n == 4:
                    act.wait_ge(p_gate.sem, p_gate.at(s))
                    fn(gth[:, :], bM[:, 0:NT * E], ACT.Tanh, scale=0.5).then_inc(a_gate.sem, 1)

            def body(s, A, B, C):
                a, c = s.plus(1), s.plus(-1)
                for k in range(PAIRS + 1):
                    h = 2 * k
                    heads = B and h < HEADS
                    if heads:
                        exps(s, h)
                    if C and k < PAIRS:
                        act.wait_ge(p_g.sem, p_g.at(c, k + 1))
                        fn(flat(tg[:, :, :]), bG[:, :], ACT.Tanh, scale=0.5).then_inc(a_tg.sem, 1)
                    if B and 0 < h <= HEADS:
                        copy_probs(s, h - 1)
                    if heads:
                        exps(s, h + 1)
                        copy_probs(s, h)
                    if A and k < 8:
                        a_chunk(a, k)
                if B:
                    for n in range(5):
                        b_tail(s, n)

            bodies(act, body)

        @block.vector
        def _(dve):
            stt, tt, ts = dve.scalar_tensor_tensor, dve.tensor_tensor, dve.tensor_scalar
            M = cols(bM)

            def flat(t):
                return t.rearrange("p a b -> p (a b)")

            def norm(n, s, src, dst, done):
                for t in range(NT):
                    last = dve.bn_stats(st[:, n, t, :], src[:, t, :])
                last.then_inc(d_st[n].sem, 1)
                dve.wait_ge(s_zero, 1)
                dve.wait_ge(d_st[n].sem, d_st[n].at(s))
                for t in range(NT):
                    last = dve.bn_aggr(mv[:, n, t, :], st[:, n, t, :])
                last.then_inc(d_mv[n].sem, 1)
                dve.wait_ge(d_mv[n].sem, d_mv[n].at(s))
                ts(vpe[:, n, :], mv[:, n, :, 1], EPS, None, ALU.add).then_inc(d_vpe[n].sem, 1)
                dve.wait_ge(g_rstd[n].sem, g_rstd[n].at(s))
                for t in range(NT):
                    last = ts(dst[:, t, :], src[:, t, :], mv[:, n, t, 0:1], rstd[:, n, t:t + 1], ALU.subtract, ALU.mult)
                last.then_inc(done.sem, 1)

            dve.memset(xTs[:, 1], 0.0)
            dve.memset(Sd[:, :, :], 0.0)
            dve.memset(Sn[:, :, :], 0.0)
            dve.memset(mhalf[:, :], -0.5)
            dve.memset(Vz[:, :, :], 0.0).then_inc(s_zero, 1)
            dve.wait_ge(s_const, 16 * 8)
            ts(qscale[:, :], par_mask[:, :], SCALE, None, ALU.mult).then_inc(s_qs, 1)
            dve.wait_ge(s_zero, 1)
            dve.wait_ge(s_qs, 1)
            for hp in range(2):
                last = ts(qbias[:, hp, :], vec[:, 5, :], qscale[:, hp:hp + 1], None, ALU.mult)
            last.then_inc(s_qb, 1)
            dve.wait_ge(s_decay, 1)

            def a_chunk(s, n):
                if n == 0:
                    dve.wait_ge(s_in[s.par], 48 * (s.half + 1))
                    now, before = xTs[:, s.par], xTs[:, 1 - s.par]
                    tt(dx[:, :, :], now, before, ALU.subtract).then_inc(d_dx.sem, 1)
                    dve.wait_ge(d_dx.sem, d_dx.at(s))
                    for m in range(3):
                        for j in range(ND):
                            last = stt(mix[:, m, j, :], dx[:, j, :], vec[:, m, j:j + 1], before[:, j, :], ALU.mult, ALU.add)
                        last.then_inc(d_mix.sem, 1)
                elif n == 1:
                    dve.wait_ge(p_kvr.sem, p_kvr.at(s, 2))
                    dve.wait_ge(a_ek.sem, a_ek.at(s))
                    tt(ekv[:, :, :], ek[:, :, :], M, ALU.mult).then_inc(d_ekv.sem, 1)
                    for j in range(ND):
                        last = stt(den[:, j, :], ek[:, j, :], eu[:, j:j + 1], Sd[:, j, :], ALU.mult, ALU.add)
                    last.then_inc(d_den.sem, 1)
                    dve.wait_ge(d_ekv.sem, d_ekv.at(s))
                    for j in range(ND):
                        last = stt(num[:, j, :], ekv[:, j, :], eu[:, j:j + 1], Sn[:, j, :], ALU.mult, ALU.add)
                    last.then_inc(d_den.sem, 1)
                elif n == 2:
                    dve.wait_ge(d_den.sem, d_den.at(s))
                    for j in range(ND):
                        last = stt(Sd[:, j, :], Sd[:, j, :], decay[:, j:j + 1], ek[:, j, :], ALU.mult, ALU.add)
                    last.then_inc(d_state.sem, 1)
                    for j in range(ND):
                        last = stt(Sn[:, j, :], Sn[:, j, :], decay[:, j:j + 1], ekv[:, j, :], ALU.mult, ALU.add)
                    last.then_inc(d_state.sem, 1)
                elif n == 3:
                    dve.wait_ge(a_thr.sem, a_thr.at(s))
                    dve.reciprocal(flat(den[:, :, :]), flat(den[:, :, :])).then_inc(d_wkv.sem, 1)
                    stt(flat(num[:, :, :]), flat(thr[:, :, :]), 1.0, flat(num[:, :, :]), ALU.add, ALU.mult).then_inc(d_num2.sem, 1)
                    dve.wait_ge(d_wkv.sem, d_wkv.at(s, 1))
                    dve.wait_ge(d_num2.sem, d_num2.at(s))
                    tt(wkv[:, :, :], num[:, :, :], den[:, :, :], ALU.mult).then_inc(d_wkv.sem, 1)
                elif n == 5:
                    dve.wait_ge(p_wout.sem, p_wout.at(s))
                    stt(z1[:, :, :], M, 0.5, xs[:, s.par], ALU.mult, ALU.add).then_inc(d_z1.sem, 1)
                    dve.wait_ge(d_z1.sem, d_z1.at(s))
                    norm(0, s, z1, x1, d_x1)

            d_num2 = event("d_num2")

            def clip(s, h):
                dve.wait_ge(p_s.sem, p_s.at(s, h + 1))
                if h >= 2:
                    dve.wait_ge(a_exp.sem, a_exp.at(s, h - 1))
                ts(flat(Sc[:, h % 2]), bS[:, :], CLAMP, -CLAMP, ALU.min, ALU.max).then_inc(d_clip.sem, 1)
                dve.wait_ge(d_clip.sem, d_clip.at(s, h + 1))
                dve.tensor_reduce(nmx[:, h, :], Sc[:, h % 2], AX.X, ALU.max, negate=True).then_inc(d_max.sem, 1)

            def b_tail(s, n):
                if n == 0:
                    dve.wait_ge(a_exp.sem, a_exp.at(s))
                    dve.reciprocal(flat(rr[:, :, :]), flat(rs[:, :, :])).then_inc(d_rr.sem, 1)
                elif n == 1:
                    dve.wait_ge(a_R.sem, a_R.at(s))
                    dve.wait_ge(p_av.sem, p_av.at(s))
                    tt(aoT[:, :, :], Rb[:, :, :], cols(bO), ALU.mult).then_inc(d_ao.sem, 1)
                elif n == 2:
                    dve.wait_ge(p_wo.sem, p_wo.at(s))
                    dve.wait_ge(g_x1b.sem, g_x1b.at(s))
                    tt(z2[:, :, :], x1b[:, s.par], M, ALU.add).then_inc(d_z2.sem, 1)
                    dve.wait_ge(d_z2.sem, d_z2.at(s))
                    norm(1, s, z2, x2[:, s.par], d_x2)
                elif n == 4:
                    dve.wait_ge(a_gate.sem, a_gate.at(s))
                    router(s)

            def router(s):
                step = [0]

                def did(ins):
                    step[0] += 1
                    ins.then_inc(d_gate.sem, 1)
                    return step[0]

                def after(k):
                    dve.wait_ge(d_gate.sem, d_gate.at(s, k))

                after(did(ts(flat(sc[:, :, :]), gth[:, :], 0.5, 0.5, ALU.mult, ALU.add)))
                v = sc[:, :, :].rearrange("p t (g e) -> p (t g) e", e=EG)
                for n, (i, j) in enumerate([(0, 1), (0, 2), (0, 3), (1, 2), (1, 3), (2, 3)]):
                    last = tt(pair[:, :, n:n + 1], v[:, :, i:i + 1], v[:, :, j:j + 1], ALU.add)
                after(did(last))
                after(did(dve.tensor_reduce(gsum[:, :, :].rearrange("p t g -> p (t g)"), pair[:, :, :], AX.X, ALU.max)))

                def ranks(val, gt, eq, rank, n):
                    for t in range(NT):
                        vj = val[:, t, :].rearrange("p (a e) -> p a e", a=1).to_broadcast([P, n, n])
                        vi = val[:, t, :].rearrange("p (e a) -> p e a", a=1).to_broadcast([P, n, n])
                        tt(gt[:, t], vj, vi, ALU.is_gt)
                        last = tt(eq[:, t], vj, vi, ALU.is_equal)
                    k = did(last)
                    after(k)
                    for t in range(NT):
                        last = tt(eq[:, t], eq[:, t], lower[:, 0:n, 0:n], ALU.mult)
                    after(did(last))
                    after(did(tt(gt.rearrange("p t i j -> p (t i j)"), gt.rearrange("p t i j -> p (t i j)"),
                                 eq.rearrange("p t i j -> p (t i j)"), ALU.add)))
                    after(did(dve.tensor_reduce(rank, gt.rearrange("p t i j -> p (t i) j"), AX.X, ALU.add)))

                ranks(gsum, ggt[:, :, :, :], geq[:, :, :, :], grank[:, :, :].rearrange("p t g -> p (t g)"), GROUPS)
                after(did(ts(gok[:, :, :], grank[:, :, :], float(TOPG) - 0.5, 2.0, ALU.is_lt, ALU.mult)))
                m4 = msk[:, :, :].rearrange("p t (g e) -> p (t g) e", e=EG)
                g4 = gok[:, :, :].rearrange("p t (g a) -> p (t g) a", a=1).to_broadcast([P, NT * GROUPS, EG])
                after(did(tt(m4, v, g4, ALU.mult)))
                ranks(msk, egt[:, :, :, :], eeq[:, :, :, :], erank[:, :, :].rearrange("p t e -> p (t e)"), E)
                for t in range(NT):
                    last = stt(wsel[:, t, :], erank[:, t, :], float(TOPK) - 0.5, sc[:, t, :], ALU.is_lt, ALU.mult,
                               accum_out=wsum[:, t:t + 1])
                last.then_inc(d_wsel.sem, 1)
                dve.wait_ge(d_wsel.sem, d_wsel.at(s))
                ts(wrec[:, :], wsum[:, :], 1e-6, 2.0, ALU.add, ALU.mult).then_inc(d_wsel2.sem, 1)
                dve.wait_ge(d_wsel2.sem, d_wsel2.at(s))
                dve.reciprocal(wrec[:, :], wrec[:, :]).then_inc(d_wsel3.sem, 1)
                dve.wait_ge(d_wsel3.sem, d_wsel3.at(s))
                for t in range(NT):
                    last = ts(comb[:, s.par, t, :], wsel[:, t, :], wrec[:, t:t + 1], None, ALU.mult)
                last.then_inc(d_comb.sem, 1)
                assert step[0] == d_gate.per, step[0]

            d_wsel, d_wsel2, d_wsel3, d_comb = (event(n) for n in ("d_wsel", "d_wsel2", "d_wsel3", "d_comb"))

            def hidden(s, k):
                if k:
                    dve.wait_ge(d_h.sem, d_h.at(s, k))
                elif not first(s):
                    dve.wait_ge(d_h.sem, d_h.at(s.plus(-1)))
                dve.wait_ge(a_tg.sem, a_tg.at(s, k + 1))
                stt(flat(t1[:, :, :]), flat(tg[:, :, :]), 1.0, bG[:, :], ALU.add, ALU.mult).then_inc(d_t1.sem, 1)
                dve.wait_ge(d_t1.sem, d_t1.at(s, k + 1))
                dve.wait_ge(p_u.sem, p_u.at(s, k + 1))
                if k >= 2:
                    dve.wait_ge(p_y.sem, p_y.at(s, max(1, 2 * k - 3)))
                elif not first(s):
                    dve.wait_ge(p_y.sem, p_y.at(s.plus(-1)))
                tt(flat(hid[:, k % 2]), flat(t1[:, :, :]), bU[:, :], ALU.mult).then_inc(d_h.sem, 1)

            def gather(s, k, i):
                if k == 0:
                    dve.wait_ge(p_y.sem, p_y.at(s, 1))
                    if not first(s):
                        dve.wait_ge(d_yo.sem, d_yo.at(s.plus(-1)))
                    stt(acc[:, :, :], cols(bY0), 0.5, x2[:, s.par], ALU.mult, ALU.add).then_inc(d_acc.sem, 1)
                    return
                if k == 1 and i == 0:
                    dve.wait_ge(d_comb.sem, d_comb.at(s))
                dve.wait_ge(p_y.sem, p_y.at(s, 2 * k + i))
                dve.wait_ge(d_acc.sem, d_acc.at(s, 2 * k + i - 1))
                for t in range(NT):
                    e = 2 * (k - 1) + i
                    last = stt(acc[:, t, :], cols(bY[i])[:, t, :], comb[:, s.par, t, e:e + 1], acc[:, t, :], ALU.mult, ALU.add)
                last.then_inc(d_acc.sem, 1)

            def body(s, A, B, C):
                a, c = s.plus(1), s.plus(-1)
                for k in range(PAIRS + 1):
                    h = 2 * k
                    heads = B and h < HEADS
                    if heads:
                        clip(s, h)
                    if C and k < PAIRS:
                        hidden(c, k)
                    if heads:
                        clip(s, h + 1)
                    if C and k:
                        gather(c, k - 1, 0)
                        if k > 1:
                            gather(c, k - 1, 1)
                    if A and k < 8:
                        a_chunk(a, k)
                if B:
                    for n in range(4):
                        b_tail(s, n)
                if C:
                    dve.wait_ge(d_acc.sem, d_acc.at(c))
                    if not (isinstance(c.l, int) and c.l < 2):
                        dve.wait_ge(s_out[c.par], 16 * c.half)
                    norm(2, c, acc, yo[:, c.par], d_yo)
                if B:
                    b_tail(s, 4)

            bodies(dve, body)

        @block.gpsimd
        def _(pool):
            def rsqrt(n, s):
                pool.wait_ge(d_vpe[n].sem, d_vpe[n].at(s))
                pool.tensor_tensor(rstd[:, n, :], vpe[:, n, :], mhalf[:, :], ALU.pow).then_inc(g_rstd[n].sem, 1)

            def body(s, A, B, C):
                a, c = s.plus(1), s.plus(-1)
                if A:
                    rsqrt(0, a)
                    pool.wait_ge(d_x1.sem, d_x1.at(a))
                    for t in range(NT):
                        last = pool.tensor_tensor(x1b[:, a.par, t, :], x1[:, t, :], bo_row[:, :], ALU.add)
                    last.then_inc(g_x1b.sem, 1)
                if B:
                    rsqrt(1, s)
                if A:
                    pool.wait_ge(a_v.sem, a_v.at(a))
                    if B:
                        pool.wait_ge(p_av.sem, p_av.at(s))
                    for t in range(NT):
                        dst = Vz[:, t, :].rearrange("p (m c) -> p m c", c=P + HD)[:, :, 0:HD]
                        last = pool.tensor_tensor(dst, Vs[:, t, :].rearrange("p (m c) -> p m c", c=HD),
                                                  bv_row[:, :].rearrange("p (m c) -> p m c", c=HD), ALU.add)
                    last.then_inc(g_v.sem, 1)
                if C:
                    rsqrt(2, c)

            pool.wait_ge(s_zero, 1)
            pool.wait_ge(s_const, 16 * 8)
            bodies(pool, body)


def kernel(**inputs):
    import concourse.bacc as _bacc
    from concourse.bass_utils import run_bass_kernel_spmd as _run

    a = {k: np.asarray(v) for k, v in inputs.items()}
    at, xa, ff = "L0_attn_", "L0_xattn_", "L0_ffn_"

    def column(v):
        return v.reshape(ND, P).T

    p = np.arange(P)
    arrays = {
        "x": a["x"],
        "xT": a["x"].transpose(0, 2, 1),
        "ctxT": a["ctx_768"].transpose(0, 2, 1),
        "vecs": np.stack([column(a[at + "mu_k"]), column(a[at + "mu_v"]), column(a[at + "mu_r"]), column(a[at + "w"]),
                          column(a[at + "u"]), column(a[xa + "bq"]), column(a[xa + "bk"])], axis=1),
        "rows": np.stack([np.broadcast_to(a[xa + "bv"], (P, D)), np.broadcast_to(a[xa + "bo"], (P, D))]),
        "wproj": np.stack([a[at + "Wk"].T, a[at + "Wv"].T, a[at + "Wr"].T, a[at + "W_out"].T, a[xa + "Wq"], a[xa + "Wo"]]),
        "wctx": np.stack([a[xa + "Wk"], a[xa + "Wv"]]),
        "w1": np.concatenate([a[ff + "w1_s"], a[ff + "w1_e"].reshape(E * F, D)]).T,
        "w3": np.concatenate([a[ff + "w3_s"], a[ff + "w3_e"].reshape(E * F, D)]).T,
        "w2": np.concatenate([a[ff + "w2_s"].T.reshape(2, P, D), a[ff + "w2_e"].transpose(0, 2, 1)]),
        "wg": a[ff + "w_gate"].T,
        "ident": np.eye(P, dtype=np.float32),
        "sel": (np.arange(HEADS)[:, None, None] == HG * np.arange(ND)[None, :, None] + p[None, None, :] // HD).astype(np.float32),
        "parity": np.stack([p // HD % 2 == 0, p // HD % 2 == 1], axis=1).astype(np.float32),
        "below": np.ascontiguousarray(np.broadcast_to(np.tril(np.ones((E, E), np.float32), -1), (P, E, E))),
    }
    nc = _bacc.Bacc("TRN2", target_bir_lowering=False, num_devices=1)
    args = []
    for name, v in arrays.items():
        arrays[name] = v = np.ascontiguousarray(v)
        args.append(nc.dram_tensor(name, v.shape, mybir.dt.from_np(v.dtype), kind="ExternalInput").ap())
    out = nc.dram_tensor("out", (L, TOK, D), F32, kind="ExternalOutput").ap()
    decoder_layer(nc, *args, out)
    return _run(nc, [arrays], core_ids=[0]).results[0]["out"]
```

```python
from contextlib import ExitStack

import numpy as np

import concourse.bass as bass
from concourse import mybir

F32 = mybir.dt.float32
F32R = mybir.dt.float32r
ACT = mybir.ActivationFunctionType
ALU = mybir.AluOpType
AX = mybir.AxisListType

P = 128
L, TOK, D = 16, 256, 256
CKV = 192
CP = CKV // 2
NT = TOK // P
ND = D // P
HEADS, HD = 16, 16
HG = P // HD
E, F = 16, 128
GROUPS, TOPG, TOPK = 4, 2, 4
EG = E // GROUPS
PAIRS = E // 2 + 1
SCALE = float(HD) ** -0.5
CLAMP = 10000.0
EPS = 1e-5
HB = 32
HT = P // HB
NHT = HEADS // HT
WCH = 384
NWCH = 2 * PAIRS * F // WCH


class Step:

    def __init__(self, i, off):
        self.i, self.off = i, off
        self.l = 2 * i + off
        self.half = i + off // 2
        self.par = off % 2

    def plus(self, k):
        return Step(self.i, self.off + k)


class Event:

    def __init__(self, sem, per):
        self.sem, self.per = sem, per

    def at(self, step, k=None):
        return step.l * self.per + (self.per if k is None else k)


def first(step):
    return isinstance(step.l, int) and step.l == 0


TAIL_AT = [1, 2, 3, 4, 5, 6]

MIX_AT = 4
ROUTER_AT = [6, 7, 8]
ROUTER_SIGNALS = [0, 7, 13, 13]

VECS = ["mu_k", "mu_v", "mu_r", "w", "u", "bq", "bk"]


def decoder_layer(nc, x, xT, ctxT, vecs, rows, wproj, wctx, wo, w1, w3, w2, wg, ident, sel, sel2, parity, below, out):
    with ExitStack() as ctx:
        def sb(name, shape, dt=F32):
            return ctx.enter_context(nc.sbuf_tensor(name, shape, dt))

        def bank(name):
            return ctx.enter_context(nc.psum_tensor(name, [P, 512], F32))

        def sem(name):
            return ctx.enter_context(nc.semaphore(name))

        def event(name, per=1):
            return Event(sem(name), per)

        Wp = sb("Wp", [P, 5, ND, D])
        WK, WV, WR, WOUT, WQ = range(5)
        Wo = sb("Wo", [P, NHT, D])
        Wc = sb("Wc", [CP, 2, 2, D])
        W13 = sb("W13", [P, 2, 2, ND, 2 * PAIRS * F], F32R)
        late = sb("late", [P, 2 * ND * WCH])
        wraw = late[:, :].rearrange("p (r j c) -> p r j c", r=2, j=ND)
        W2 = sb("W2", [P, 2 * PAIRS, D])
        Wg = sb("Wg", [P, ND, E])
        Wgs = sb("Wgs", [P, 2, ND, E], F32R)
        idn = sb("idn", [P, P])
        selh = sb("selh", [HEADS, NHT, P])
        sele_raw = sb("sele_raw", [2 * E, E + 1])
        sele = sb("sele", [2 * E, E], F32R)
        par_mask = sb("par_mask", [P, 2])
        lower = sb("lower", [P, E, E])
        vec = sb("vec", [P, len(VECS), ND])
        minus_low = sb("minus_low", [2 * E, 1])
        bv_row = sb("bv_row", [P, D])
        bo_row = sb("bo_row", [P, D])
        decay = sb("decay", [P, ND])
        ew = sb("ew", [P, ND])
        eu = sb("eu", [P, ND])
        qscale = sb("qscale", [P, 2])
        qbias = sb("qbias", [P, 2, ND])
        mhalf = sb("mhalf", [P, NT])

        xTs = sb("xTs", [P, 2, ND, TOK])
        xs = sb("xs", [P, NT, D])
        cT = sb("cT", [CP, 2, TOK])
        dx = sb("dx", [P, ND, TOK])
        mix = sb("mix", [P, 3, ND, TOK])
        ek = sb("ek", [P, ND, TOK])
        ekv = sb("ekv", [P, ND, TOK])
        thr = sb("thr", [P, ND, TOK])
        den = sb("den", [P, ND, TOK])
        num = sb("num", [P, ND, TOK])
        Sd = sb("Sd", [P, ND, TOK])
        Sn = sb("Sn", [P, ND, TOK])
        x1 = sb("x1", [P, NT, D])
        x1T = thr
        x1b = sb("x1b", [P, 2, NT, D])
        QT = sb("QT", [P, 2, ND, TOK])
        KT = sb("KT", [P, 2, ND, TOK])
        Vs = sb("Vs", [P, 2, NT, D + HD])

        Sc = sb("Sc", [P, 2, NT, TOK])
        nmx = sb("nmx", [P, HEADS, NT])
        Pr = sb("Pr", [P, 2, NT, TOK])
        rs = sb("rs", [P, 2, NT, HEADS])
        rr = sb("rr", [P, NT, HEADS])
        PT = sb("PT", [P, 2, NT, TOK])
        rT = sb("rT", [HEADS, TOK])
        ao = sb("ao", [P, NHT, TOK])
        gth = sb("gth", [P, NT * E])
        sc = sb("sc", [P, NT, E])
        pair = sb("pair", [P, NT * GROUPS, 6])
        gsum = sb("gsum", [P, NT, GROUPS])
        ggt = sb("ggt", [P, NT, GROUPS, GROUPS])
        geq = sb("geq", [P, NT, GROUPS, GROUPS])
        grank = sb("grank", [P, NT, GROUPS])
        gok = sb("gok", [P, NT, GROUPS])
        msk = sb("msk", [P, NT, E])
        egt = dx[:, :, :].rearrange("p t (i j) -> p t i j", i=E)
        eeq = den[:, :, :].rearrange("p t (i j) -> p t i j", i=E)
        erank = sb("erank", [P, NT, E])
        wsel = sb("wsel", [P, NT, E])
        wsum = sb("wsum", [P, NT])
        wrec = sb("wrec", [P, NT])
        x2 = sb("x2", [P, 2, NT, D])
        x2T = sb("x2T", [P, 2, 2, ND, TOK], F32R)
        comb = sb("comb", [P, NT, 2, E])
        combh = sb("combh", [2 * E, TOK], F32R)
        combT = sb("combT", [2 * E, 2, TOK], F32R)

        yo = late[:, 0:2 * NT * D].rearrange("p (r t d) -> p r t d", r=2, t=NT)
        tg = late[:, 2 * NT * D:].rearrange("p (i t) -> p i t", i=2)
        hid = sb("hid", [P, 2, 2, TOK])

        st = sb("st", [P, 3, NT, 6])
        mv = sb("mv", [P, 3, NT, 2])
        vpe = sb("vpe", [P, 3, NT])
        rstd = sb("rstd", [P, 3, NT])

        bG, bU, bC, bY, bS, bT, bO, bM = (bank(n) for n in ("bG", "bU", "bC", "bY", "bS", "bT", "bO", "bM"))

        def cols(b, n=2):
            return b[:, :].rearrange("p (n c) -> p n c", n=n)

        s_att = sem("s_att")
        s_w2 = sem("s_w2")
        s_raw = [sem("s_raw0"), sem("s_raw1")]
        s_high = sem("s_high")
        s_split = sem("s_split")
        s_small = sem("s_small")
        s_const = sem("s_const")
        s_zero = sem("s_zero")
        s_ew = sem("s_ew")
        s_decay = sem("s_decay")
        s_qs = sem("s_qs")
        s_qb = sem("s_qb")
        s_xT = [sem("s_xT0"), sem("s_xT1")]
        s_x = sem("s_x")
        s_ctx = sem("s_ctx")
        s_out = [sem("s_out0"), sem("s_out1")]
        d_dx = event("d_dx")
        d_mix = event("d_mix", 3)
        p_kvr = event("p_kvr", 3)
        a_ek = event("a_ek")
        d_ekv = event("d_ekv")
        a_thr = event("a_thr")
        d_den = event("d_den", 2)
        d_state = event("d_state", 2)
        d_rden = event("d_rden")
        d_num = event("d_num")
        d_wkv = event("d_wkv")
        p_wout = event("p_wout")
        d_z1 = event("d_z1")
        d_x1 = event("d_x1")
        g_x1b = event("g_x1b")
        p_x1T = event("p_x1T")
        a_x1T = event("a_x1T")
        p_q = event("p_q")
        a_q = event("a_q")
        p_k = event("p_k")
        a_k = event("a_k")
        p_v = event("p_v")
        d_v = event("d_v")
        d_st = [event(f"d_st{n}") for n in range(3)]
        d_mv = [event(f"d_mv{n}") for n in range(3)]
        d_vpe = [event(f"d_vpe{n}") for n in range(3)]
        g_rstd = [event(f"g_rstd{n}") for n in range(3)]
        p_s = event("p_s", HEADS)
        d_clip = event("d_clip", HEADS)
        d_max = event("d_max", HEADS)
        a_exp = event("a_exp", HEADS)
        p_t = event("p_t", HEADS)
        a_pt = event("a_pt", HEADS)
        p_av = event("p_av", HEADS)
        a_o = event("a_o", 2)
        d_rr = event("d_rr")
        p_rT = event("p_rT")
        a_rT = event("a_rT")
        p_R = event("p_R", 2)
        d_ao = event("d_ao", 2)
        p_wo = event("p_wo")
        d_z2 = event("d_z2")
        d_x2 = event("d_x2")
        p_x2T = event("p_x2T")
        a_x2T = event("a_x2T")
        d_x2T = event("d_x2T")
        p_gate = event("p_gate")
        a_gate = event("a_gate")
        d_gate = event("d_gate", ROUTER_SIGNALS[-1])
        d_wsel = event("d_wsel")
        d_wsum = event("d_wsum")
        d_wrec = event("d_wrec")
        d_comb = event("d_comb")
        p_comb = event("p_comb")
        a_comb = event("a_comb")
        d_combT = event("d_combT")
        p_g = event("p_g", PAIRS)
        p_u = event("p_u", PAIRS)
        p_c = event("p_c", PAIRS - 1)
        a_tg = event("a_tg", PAIRS)
        d_t1 = event("d_t1", PAIRS)
        d_t2 = event("d_t2", PAIRS)
        d_t3 = event("d_t3", PAIRS - 1)
        p_y = event("p_y", PAIRS)
        d_z3 = event("d_z3")
        d_yo = event("d_yo")

        block = ctx.enter_context(nc.Block())

        def last_bodies(body):
            body(Step(L // 2, -1), B=True, T=True, C=True, F=True)
            body(Step(L // 2, 0), T=True, C=True, F=True)
            body(Step(L // 2, 1), C=True, F=True)
            body(Step(L // 2, 2), F=True)

        def bodies(eng, body):
            body(Step(0, -1), A=True)
            body(Step(0, 0), A=True, B=True)
            body(Step(0, 1), A=True, B=True, T=True)
            body(Step(0, 2), A=True, B=True, T=True, C=True)
            with eng.Fori(1, (L - 2) // 2) as i:
                body(Step(i, 1), A=True, B=True, T=True, C=True, F=True)
                body(Step(i, 2), A=True, B=True, T=True, C=True, F=True)
            last_bodies(body)

        @block.sync
        def _(sp):
            def load(step):
                p = step.par
                if not first(step):
                    sp.wait_ge(d_mix.sem, d_mix.at(step.plus(-1)))
                sp.dma_start(xTs[:, p], xT[bass.ds(step.l, 1)].rearrange("a (j p) t -> p (a j) t", p=P)).then_inc(s_xT[p], 16)
                if not first(step):
                    sp.wait_ge(p_v.sem, p_v.at(step.plus(-1)))
                sp.dma_start(cT[:, :, :], ctxT[bass.ds(step.l, 1)].rearrange("a (j p) t -> p (a j) t", p=CP)).then_inc(s_ctx, 16)
                if not first(step):
                    sp.wait_ge(d_z1.sem, d_z1.at(step.plus(-1)))
                sp.dma_start(xs[:, :, :], x[bass.ds(step.l, 1)].rearrange("a (t p) d -> p (a t) d", p=P)).then_inc(s_x, 16)

            sp.dma_start(vec[:, :, :], vecs).then_inc(s_const, 16)
            sp.dma_start(par_mask[:, :], parity).then_inc(s_const, 16)
            load(Step(0, 0))
            sp.dma_start(Wp[:, :, :, :], wproj.rearrange("w (j p) d -> p w j d", p=P)).then_inc(s_att, 16)
            sp.dma_start(Wc[:, :, :, :], wctx.rearrange("w (j p) d -> p w j d", p=CP)).then_inc(s_att, 16)
            sp.dma_start(idn[:, :], ident).then_inc(s_const, 16)
            sp.dma_start(bv_row[:, :], rows[0]).then_inc(s_const, 16)
            sp.dma_start(bo_row[:, :], rows[1]).then_inc(s_const, 16)
            sp.dma_start(selh[:, :, :], sel).then_inc(s_const, 16)
            sp.dma_start(sele_raw[:, :], sel2).then_inc(s_const, 16)
            sp.dma_start(lower[:, :, :], below).then_inc(s_const, 16)
            sp.dma_start(Wg[:, :, :], wg.rearrange("(j p) e -> p j e", p=P)).then_inc(s_const, 16)
            sp.dma_start(Wo[:, :, :], wo.rearrange("c p h -> p c h")).then_inc(s_att, 16)

            def body(s, A=False, B=False, T=False, C=False, F=False):
                a, f = s.plus(1), s.plus(-3)
                if A and not (isinstance(a.l, int) and a.l == L - 1):
                    load(a.plus(1))
                if F:
                    sp.wait_ge(d_yo.sem, d_yo.at(f))
                    sp.dma_start(out[bass.ds(f.l, 1)].rearrange("a (t p) d -> p (a t) d", p=P), yo[:, f.par]).then_inc(s_out[f.par], 16)

            def load_experts(w, src):
                for n in range(w * NWCH, (w + 1) * NWCH):
                    if n >= 2:
                        sp.wait_ge(s_split, n - 1)
                    c = (n - w * NWCH) * WCH
                    sp.dma_start(wraw[:, n % 2], src[:, c:c + WCH].rearrange("(j p) f -> p j f", p=P)).then_inc(s_raw[n % 2], 16)

            body(Step(0, -1), A=True)
            load_experts(0, w1)
            body(Step(0, 0), A=True, B=True)
            load_experts(1, w3)
            sp.dma_start(W2[:, :, :], w2.rearrange("c p h -> p c h")).then_inc(s_w2, 16)
            body(Step(0, 1), A=True, B=True, T=True)
            body(Step(0, 2), A=True, B=True, T=True, C=True)
            with sp.Fori(1, (L - 4) // 2) as i:
                body(Step(i, 1), A=True, B=True, T=True, C=True, F=True)
                body(Step(i, 2), A=True, B=True, T=True, C=True, F=True)
            body(Step((L - 4) // 2, 1), A=True, B=True, T=True, C=True, F=True)
            body(Step((L - 4) // 2, 2), A=True, B=True, T=True, C=True, F=True)
            last_bodies(body)
            for p in range(2):
                sp.wait_ge(s_out[p], 16 * L // 2)

        @block.tensor
        def _(pe):
            mm = pe.matmul

            def proj(dst, w, src, n):
                for m in range(ND):
                    for j in range(n):
                        last = mm(dst[:, m, :], w[:, j, m * P:(m + 1) * P], src[:, j, :], start=(j == 0), stop=(j == n - 1))
                return last

            def token_proj(dst, w, src, n):
                for t in range(NT):
                    for j in range(n):
                        last = mm(dst[:, t, :], src[:, j, t * P:(t + 1) * P], w[:, j, :], start=(j == 0), stop=(j == n - 1))
                return last

            def turn(dst, src):
                for j in range(ND):
                    for t in range(NT):
                        last = pe.transpose(dst[:, j, t * P:(t + 1) * P], src[:, t, j * P:(j + 1) * P], idn[:, :])
                return last

            M = cols(bM)

            def split(dst, w, x, js, start=True, stop=True):
                terms = [(j, a, b) for j in js for a, b in ((0, 0), (0, 1), (1, 0))]
                for n, (j, a, b) in enumerate(terms):
                    last = mm(dst, w(a, j), x(b, j), start=(start and n == 0), stop=(stop and n == len(terms) - 1))
                return last

            def a_chunk(s, n, t, c):
                if n == 0:
                    if first(s):
                        pe.wait_ge(s_att, 48)
                    elif c is not None:
                        pe.wait_ge(d_combT.sem, d_combT.at(c))
                    else:
                        pe.wait_ge(a_q.sem, a_q.at(s.plus(-1)))
                    pe.wait_ge(d_mix.sem, d_mix.at(s, 1))
                    proj(M, Wp[:, WK], mix[:, 0], ND).then_inc(p_kvr.sem, 1)
                elif n == 1:
                    pe.wait_ge(d_mix.sem, d_mix.at(s, 2))
                    pe.wait_ge(a_ek.sem, a_ek.at(s))
                    if t is not None:
                        pe.wait_ge(a_rT.sem, a_rT.at(t))
                    proj(M, Wp[:, WV], mix[:, 1], ND).then_inc(p_kvr.sem, 1)
                elif n == 2:
                    pe.wait_ge(d_mix.sem, d_mix.at(s, 3))
                    pe.wait_ge(d_ekv.sem, d_ekv.at(s))
                    if t is not None:
                        pe.wait_ge(d_ao.sem, d_ao.at(t, 1))
                    proj(M, Wp[:, WR], mix[:, 2], ND).then_inc(p_kvr.sem, 1)
                elif n == 3:
                    pe.wait_ge(s_ctx, 16 * (s.l + 1))
                    pe.wait_ge(a_thr.sem, a_thr.at(s))
                    if t is not None:
                        pe.wait_ge(d_ao.sem, d_ao.at(t, 2))
                    proj(M, Wc[:, 0], cT, 2).then_inc(p_k.sem, 1)
                elif n == 4:
                    pe.wait_ge(a_k.sem, a_k.at(s))
                    if t is not None:
                        pe.wait_ge(d_z2.sem, d_z2.at(t))
                    token_proj(M, Wc[:, 1], cT, 2).then_inc(p_v.sem, 1)
                elif n == 5:
                    pe.wait_ge(d_v.sem, d_v.at(s))
                    if t is not None:
                        pe.wait_ge(d_x2T.sem, d_x2T.at(t))
                    pe.wait_ge(d_wkv.sem, d_wkv.at(s))
                    token_proj(M, Wp[:, WOUT], num, ND).then_inc(p_wout.sem, 1)
                elif n == 6:
                    pe.wait_ge(d_x1.sem, d_x1.at(s))
                    if t is not None:
                        pe.wait_ge(a_gate.sem, a_gate.at(t))
                    turn(M, x1).then_inc(p_x1T.sem, 1)
                elif n == 7:
                    pe.wait_ge(a_x1T.sem, a_x1T.at(s))
                    proj(M, Wp[:, WQ], x1T, ND).then_inc(p_q.sem, 1)

            def t_chunk(s, n, a):
                if n == 0:
                    if a is not None:
                        pe.wait_ge(a_ek.sem, a_ek.at(a))
                    else:
                        pe.wait_ge(d_combT.sem, d_combT.at(s.plus(-1)))
                    pe.wait_ge(d_rr.sem, d_rr.at(s))
                    for t in range(NT):
                        last = pe.transpose(bM[0:HEADS, t * P:(t + 1) * P], rr[:, t, :], idn[:, :])
                    last.then_inc(p_rT.sem, 1)
                elif n in (1, 2):
                    pe.wait_ge(a_rT.sem, a_rT.at(s))
                    if n == 1 and a is not None:
                        pe.wait_ge(d_ekv.sem, d_ekv.at(a))
                    elif n == 2 and a is not None:
                        pe.wait_ge(a_thr.sem, a_thr.at(a))
                    elif n == 2:
                        pe.wait_ge(d_ao.sem, d_ao.at(s, 1))
                    for i in range(2):
                        last = mm(M[:, i, :], selh[:, 2 * (n - 1) + i, :], rT[:, :], start=True, stop=True)
                    last.then_inc(p_R.sem, 1)
                elif n == 3:
                    if a is not None:
                        pe.wait_ge(a_k.sem, a_k.at(a))
                    pe.wait_ge(d_ao.sem, d_ao.at(s))
                    token_proj(M, Wo, ao, NHT).then_inc(p_wo.sem, 1)
                elif n == 4:
                    if a is not None:
                        pe.wait_ge(d_v.sem, d_v.at(a))
                    pe.wait_ge(d_x2.sem, d_x2.at(s))
                    turn(M, x2[:, s.par]).then_inc(p_x2T.sem, 1)
                elif n == 5:
                    if a is not None:
                        pe.wait_ge(d_z1.sem, d_z1.at(a))
                    pe.wait_ge(d_x2T.sem, d_x2T.at(s))
                    for t in range(NT):
                        last = split(bM[:, t * E:(t + 1) * E], lambda a, j: x2T[:, s.par, a, j, t * P:(t + 1) * P],
                                     lambda b, j: Wgs[:, b, j, :], range(ND))
                    last.then_inc(p_gate.sem, 1)

            def turn_combine(s, a):
                if a is not None:
                    pe.wait_ge(a_q.sem, a_q.at(a))
                else:
                    pe.wait_ge(a_gate.sem, a_gate.at(s))
                pe.wait_ge(d_comb.sem, d_comb.at(s))
                for t in range(NT):
                    last = pe.transpose(bM[0:2 * E, t * P:(t + 1) * P], comb[:, t].rearrange("p a e -> p (a e)"), idn[:, :])
                last.then_inc(p_comb.sem, 1)

            def scores(s, h):
                g, m = divmod(h, HG)
                r = 32 * (m // 2)
                if h == 0:
                    pe.wait_ge(a_q.sem, a_q.at(s))
                    pe.wait_ge(a_k.sem, a_k.at(s))
                    if not first(s):
                        pe.wait_ge(d_clip.sem, d_clip.at(s.plus(-1)))
                else:
                    pe.wait_ge(d_clip.sem, d_clip.at(s, h))
                S = cols(bS)
                for t in range(NT):
                    last = mm(S[:, t, :], QT[r:r + 32, m % 2, g, t * P:(t + 1) * P], KT[r:r + 32, s.par, g, :], start=True, stop=True)
                last.then_inc(p_s.sem, 1)

            def turn_probs(s, h):
                pe.wait_ge(a_exp.sem, a_exp.at(s, h + 1))
                if h:
                    pe.wait_ge(a_pt.sem, a_pt.at(s, h))
                turn(cols(bT), Pr[:, h % 2]).then_inc(p_t.sem, 1)

            def values(s, h):
                pe.wait_ge(a_pt.sem, a_pt.at(s, h + 1))
                if h == 0:
                    pe.wait_ge(d_v.sem, d_v.at(s))
                    if not first(s):
                        pe.wait_ge(a_o.sem, a_o.at(s.plus(-1)))
                elif h == HEADS // 2:
                    pe.wait_ge(a_o.sem, a_o.at(s, 1))
                i, c = divmod(h % (HEADS // 2), HT)
                for k in range(NT):
                    last = mm(cols(bO)[HB * c:HB * (c + 1), i, :], Vs[:, s.par, k, h * HD:h * HD + HB], PT[:, h % 2, k, :],
                              start=(k == 0), stop=(k == NT - 1))
                last.then_inc(p_av.sem, 1)

            def gate(s, k):
                if k == 0:
                    pe.wait_ge(d_x2T.sem, d_x2T.at(s))
                    if not first(s):
                        pe.wait_ge(d_t1.sem, d_t1.at(s.plus(-1)))
                else:
                    pe.wait_ge(d_t1.sem, d_t1.at(s, k))
                for i in range(2):
                    c = (2 * k + i) * F
                    last = split(cols(bG)[:, i, :], lambda a, j: W13[:, 0, a, j, c:c + F], lambda b, j: x2T[:, s.par, b, j, :], range(ND))
                last.then_inc(p_g.sem, 1)

            def up(s, k):
                if k:
                    pe.wait_ge(d_t2.sem, d_t2.at(s, k))
                elif not first(s):
                    pe.wait_ge(d_t2.sem, d_t2.at(s.plus(-1)))
                for i in range(2):
                    c = (2 * k + i) * F
                    last = split(cols(bU)[:, i, :], lambda a, j: W13[:, 1, a, j, c:c + F], lambda b, j: x2T[:, s.par, b, j, :], range(ND))
                last.then_inc(p_u.sem, 1)

            def combine(s, k):
                if k == 1:
                    pe.wait_ge(d_combT.sem, d_combT.at(s))
                    if not first(s):
                        pe.wait_ge(d_t3.sem, d_t3.at(s.plus(-1)))
                else:
                    pe.wait_ge(d_t3.sem, d_t3.at(s, k - 1))
                for i in range(2):
                    e = 2 * (k - 1) + i
                    last = mm(cols(bC)[:, i, :], sele[:, e:e + 1].to_broadcast([2 * E, P]), combT[:, s.par, :], start=True, stop=True)
                last.then_inc(p_c.sem, 1)

            def down(s, k):
                if k == 0:
                    pe.wait_ge(d_t2.sem, d_t2.at(s, 1))
                    if not first(s):
                        pe.wait_ge(d_z3.sem, d_z3.at(s.plus(-1)))
                else:
                    pe.wait_ge(d_t3.sem, d_t3.at(s, k))
                for t in range(NT):
                    for c in range(2):
                        last = mm(cols(bY)[:, t, :], hid[:, k % 2, c, t * P:(t + 1) * P], W2[:, 2 * k + c, :],
                                  start=(k == 0 and t == 0 and c == 0), stop=(k == PAIRS - 1 and c == 1), skip_group_check=True)
                last.then_inc(p_y.sem, 1)

            def body(s, A=False, B=False, T=False, C=False, F=False):
                a, t, c, f = s.plus(1), s.plus(-1), s.plus(-2), s.plus(-3)
                for k in range(PAIRS + 1):
                    h = 2 * k
                    heads = B and h < HEADS
                    if heads:
                        scores(s, h)
                    if C and k < PAIRS:
                        gate(c, k)
                    if B and 0 < h <= HEADS:
                        turn_probs(s, h - 1)
                    if C and k < PAIRS:
                        up(c, k)
                    if C and k == 0:
                        turn_combine(c, s if B else None)
                    if T and k in TAIL_AT:
                        t_chunk(t, TAIL_AT.index(k), a if A else None)
                    if B and 0 < h <= HEADS:
                        values(s, h - 1)
                    if heads:
                        scores(s, h + 1)
                    if C and 0 < k < PAIRS:
                        combine(c, k)
                    if heads:
                        turn_probs(s, h)
                    if C and k:
                        down(c, k - 1)
                    if A and k < 8:
                        a_chunk(a, k, t if T else None, c if C else None)
                    if heads:
                        values(s, h)

            pe.wait_ge(s_const, 16 * 9)
            pe.wait_ge(s_zero, 1)
            body(Step(0, -1), A=True)
            body(Step(0, 0), A=True, B=True)
            pe.wait_ge(s_small, 4)
            body(Step(0, 1), A=True, B=True, T=True)
            pe.wait_ge(s_w2, 16)
            pe.wait_ge(s_split, 2 * NWCH)
            body(Step(0, 2), A=True, B=True, T=True, C=True)
            with pe.Fori(1, (L - 2) // 2) as i:
                body(Step(i, 1), A=True, B=True, T=True, C=True, F=True)
                body(Step(i, 2), A=True, B=True, T=True, C=True, F=True)
            last_bodies(body)

        @block.scalar
        def _(act):
            fn = act.activation
            M = bM[:, :]

            def flat(t):
                return t.rearrange("p a b -> p (a b)")

            act.wait_ge(s_const, 16 * 9)
            fn(ew[:, :], vec[:, 3, :], ACT.Exp).then_inc(s_ew, 1)
            fn(eu[:, :], vec[:, 4, :], ACT.Exp)
            act.wait_ge(s_ew, 1)
            fn(decay[:, :], ew[:, :], ACT.Exp, scale=-1.0).then_inc(s_decay, 1)
            act.wait_ge(s_qb, 1)

            def a_chunk(s, n):
                if n == 0:
                    act.wait_ge(p_kvr.sem, p_kvr.at(s, 1))
                    fn(flat(ek[:, :, :]), M, ACT.Exp).then_inc(a_ek.sem, 1)
                elif n == 2:
                    act.wait_ge(p_kvr.sem, p_kvr.at(s, 3))
                    fn(flat(thr[:, :, :]), M, ACT.Tanh, scale=0.5).then_inc(a_thr.sem, 1)
                elif n == 3:
                    act.wait_ge(p_k.sem, p_k.at(s))
                    for j in range(ND):
                        last = fn(KT[:, s.par, j, :], cols(bM)[:, j, :], ACT.Identity, bias=vec[:, 6, j:j + 1])
                    last.then_inc(a_k.sem, 1)
                elif n == 6:
                    act.wait_ge(p_x1T.sem, p_x1T.at(s))
                    fn(flat(x1T[:, :, :]), M, ACT.Copy).then_inc(a_x1T.sem, 1)
                elif n == 7:
                    act.wait_ge(p_q.sem, p_q.at(s))
                    if not first(s):
                        act.wait_ge(p_s.sem, p_s.at(s.plus(-1)))
                    for hp in range(2):
                        for j in range(ND):
                            last = fn(QT[:, hp, j, :], cols(bM)[:, j, :], ACT.Identity,
                                      bias=qbias[:, hp, j:j + 1], scale=qscale[:, hp:hp + 1])
                    last.then_inc(a_q.sem, 1)

            def exps(s, h):
                act.wait_ge(d_max.sem, d_max.at(s, h + 1))
                if h >= 2:
                    act.wait_ge(p_t.sem, p_t.at(s, h - 1))
                for t in range(NT):
                    last = fn(Pr[:, h % 2, t, :], Sc[:, h % 2, t, :], ACT.Exp, bias=nmx[:, h, t:t + 1], accum_out=rs[:, s.par, t, h:h + 1])
                last.then_inc(a_exp.sem, 1)

            def copy_probs(s, h):
                act.wait_ge(p_t.sem, p_t.at(s, h + 1))
                if h >= 2:
                    act.wait_ge(p_av.sem, p_av.at(s, h - 1))
                fn(flat(PT[:, h % 2]), bT[:, :], ACT.Copy).then_inc(a_pt.sem, 1)

            def copy_out(s, half):
                act.wait_ge(p_av.sem, p_av.at(s, HEADS // 2 * (half + 1)))
                if half == 0 and not first(s):
                    act.wait_ge(p_wo.sem, p_wo.at(s.plus(-1)))
                fn(flat(ao[:, 2 * half:2 * half + 2, :]), bO[:, :], ACT.Copy).then_inc(a_o.sem, 1)

            def t_chunk(s, n):
                if n == 0:
                    act.wait_ge(p_rT.sem, p_rT.at(s))
                    fn(rT[:, :], bM[0:HEADS, 0:TOK], ACT.Copy).then_inc(a_rT.sem, 1)
                elif n == 4:
                    act.wait_ge(p_x2T.sem, p_x2T.at(s))
                    fn(flat(x2T[:, s.par, 0]), M, ACT.Copy).then_inc(a_x2T.sem, 1)
                elif n == 5:
                    act.wait_ge(p_gate.sem, p_gate.at(s))
                    fn(gth[:, :], bM[:, 0:NT * E], ACT.Tanh, scale=0.5).then_inc(a_gate.sem, 1)

            def body(s, A=False, B=False, T=False, C=False, F=False):
                a, t, c, f = s.plus(1), s.plus(-1), s.plus(-2), s.plus(-3)
                for k in range(PAIRS + 1):
                    h = 2 * k
                    heads = B and h < HEADS
                    if heads:
                        exps(s, h)
                    if C and k < PAIRS:
                        act.wait_ge(p_g.sem, p_g.at(c, k + 1))
                        if k:
                            act.wait_ge(d_t2.sem, d_t2.at(c, k))
                        elif not first(c):
                            act.wait_ge(d_t2.sem, d_t2.at(c.plus(-1)))
                        fn(flat(tg[:, :, :]), bG[:, :], ACT.Tanh, scale=0.5).then_inc(a_tg.sem, 1)
                    if B and 0 < h <= HEADS:
                        copy_probs(s, h - 1)
                    if T and k in TAIL_AT:
                        t_chunk(t, TAIL_AT.index(k))
                    if B and h in (HEADS // 2, HEADS):
                        copy_out(s, h // (HEADS // 2) - 1)
                    if C and k == 0:
                        act.wait_ge(p_comb.sem, p_comb.at(c))
                        fn(combh[:, :], bM[0:2 * E, 0:TOK], ACT.Copy).then_inc(a_comb.sem, 1)
                    if heads:
                        copy_probs(s, h)
                        exps(s, h + 1)
                    if A and k < 8:
                        a_chunk(a, k)

            bodies(act, body)

        @block.vector
        def _(dve):
            stt, tt, ts = dve.scalar_tensor_tensor, dve.tensor_tensor, dve.tensor_scalar
            M = cols(bM)

            def flat(t):
                return t.rearrange("p a b -> p (a b)")

            def norm(n, s, src, dst, done):
                for t in range(NT):
                    last = dve.bn_stats(st[:, n, t, :], src[:, t, :])
                last.then_inc(d_st[n].sem, 1)
                dve.wait_ge(s_zero, 1)
                dve.wait_ge(d_st[n].sem, d_st[n].at(s))
                for t in range(NT):
                    last = dve.bn_aggr(mv[:, n, t, :], st[:, n, t, :])
                last.then_inc(d_mv[n].sem, 1)
                dve.wait_ge(d_mv[n].sem, d_mv[n].at(s))
                ts(vpe[:, n, :], mv[:, n, :, 1], EPS, None, ALU.add).then_inc(d_vpe[n].sem, 1)
                dve.wait_ge(g_rstd[n].sem, g_rstd[n].at(s))
                for t in range(NT):
                    last = ts(dst[:, t, :], src[:, t, :], mv[:, n, t, 0:1], rstd[:, n, t:t + 1], ALU.subtract, ALU.mult)
                last.then_inc(done.sem, 1)

            dve.memset(xTs[:, 1], 0.0)
            dve.memset(Sd[:, :, :], 0.0)
            dve.memset(Sn[:, :, :], 0.0)
            dve.memset(mhalf[:, :], -0.5)
            dve.memset(Vs[:, :, :, D:D + HD], 0.0).then_inc(s_zero, 1)
            dve.wait_ge(s_const, 16 * 9)
            ts(qscale[:, :], par_mask[:, :], SCALE, None, ALU.mult).then_inc(s_qs, 1)
            dve.wait_ge(s_zero, 1)
            dve.wait_ge(s_qs, 1)
            for hp in range(2):
                last = ts(qbias[:, hp, :], vec[:, 5, :], qscale[:, hp:hp + 1], None, ALU.mult)
            last.then_inc(s_qb, 1)
            dve.tensor_copy(sele[:, :], sele_raw[:, 0:E]).then_inc(s_small, 1)
            ts(minus_low[:, :], sele_raw[:, E:E + 1], -1.0, None, ALU.mult).then_inc(s_small, 1)
            dve.tensor_copy(Wgs[:, 0], Wg[:, :, :]).then_inc(s_small, 1)
            dve.wait_ge(s_small, 3)
            tt(Wgs[:, 1], Wg[:, :, :], Wgs[:, 0].bitcast(F32), ALU.subtract).then_inc(s_small, 1)
            dve.wait_ge(s_decay, 1)

            def mixes(s):
                dve.wait_ge(s_xT[s.par], 16 * (s.half + 1))
                now, before = xTs[:, s.par], xTs[:, 1 - s.par]
                tt(dx[:, :, :], now, before, ALU.subtract).then_inc(d_dx.sem, 1)
                dve.wait_ge(d_dx.sem, d_dx.at(s))
                for m in range(3):
                    for j in range(ND):
                        last = stt(mix[:, m, j, :], dx[:, j, :], vec[:, m, j:j + 1], before[:, j, :], ALU.mult, ALU.add)
                    last.then_inc(d_mix.sem, 1)

            def a_chunk(s, n):
                if n == 1:
                    dve.wait_ge(p_kvr.sem, p_kvr.at(s, 2))
                    dve.wait_ge(a_ek.sem, a_ek.at(s))
                    tt(ekv[:, :, :], ek[:, :, :], M, ALU.mult).then_inc(d_ekv.sem, 1)
                    for j in range(ND):
                        last = stt(den[:, j, :], ek[:, j, :], eu[:, j:j + 1], Sd[:, j, :], ALU.mult, ALU.add)
                    last.then_inc(d_den.sem, 1)
                    dve.wait_ge(d_ekv.sem, d_ekv.at(s))
                    for j in range(ND):
                        last = stt(num[:, j, :], ekv[:, j, :], eu[:, j:j + 1], Sn[:, j, :], ALU.mult, ALU.add)
                    last.then_inc(d_den.sem, 1)
                elif n == 2:
                    dve.wait_ge(d_den.sem, d_den.at(s))
                    for j in range(ND):
                        last = stt(Sd[:, j, :], Sd[:, j, :], decay[:, j:j + 1], ek[:, j, :], ALU.mult, ALU.add)
                    last.then_inc(d_state.sem, 1)
                    for j in range(ND):
                        last = stt(Sn[:, j, :], Sn[:, j, :], decay[:, j:j + 1], ekv[:, j, :], ALU.mult, ALU.add)
                    last.then_inc(d_state.sem, 1)
                elif n == 3:
                    dve.wait_ge(a_thr.sem, a_thr.at(s))
                    dve.reciprocal(flat(den[:, :, :]), flat(den[:, :, :])).then_inc(d_rden.sem, 1)
                    stt(flat(num[:, :, :]), flat(thr[:, :, :]), 1.0, flat(num[:, :, :]), ALU.add, ALU.mult).then_inc(d_num.sem, 1)
                    dve.wait_ge(d_rden.sem, d_rden.at(s))
                    dve.wait_ge(d_num.sem, d_num.at(s))
                    tt(num[:, :, :], num[:, :, :], den[:, :, :], ALU.mult).then_inc(d_wkv.sem, 1)
                elif n == 4:
                    dve.wait_ge(p_v.sem, p_v.at(s))
                    for t in range(NT):
                        last = tt(Vs[:, s.par, t, 0:D], bv_row[:, :], M[:, t, :], ALU.add)
                    last.then_inc(d_v.sem, 1)
                elif n == 5:
                    dve.wait_ge(p_wout.sem, p_wout.at(s))
                    if not first(s):
                        dve.wait_ge(p_x1T.sem, p_x1T.at(s.plus(-1)))
                        dve.wait_ge(g_x1b.sem, g_x1b.at(s.plus(-1)))
                    dve.wait_ge(s_x, 16 * (s.l + 1))
                    stt(x1[:, :, :], M, 0.5, xs[:, :, :], ALU.mult, ALU.add).then_inc(d_z1.sem, 1)
                    dve.wait_ge(d_z1.sem, d_z1.at(s))
                    norm(0, s, x1, x1, d_x1)

            def clip(s, h):
                dve.wait_ge(p_s.sem, p_s.at(s, h + 1))
                if h >= 2:
                    dve.wait_ge(a_exp.sem, a_exp.at(s, h - 1))
                ts(flat(Sc[:, h % 2]), bS[:, :], CLAMP, -CLAMP, ALU.min, ALU.max).then_inc(d_clip.sem, 1)
                dve.wait_ge(d_clip.sem, d_clip.at(s, h + 1))
                dve.tensor_reduce(nmx[:, h, :], Sc[:, h % 2], AX.X, ALU.max, negate=True).then_inc(d_max.sem, 1)

            def t_chunk(s, n):
                if n == 0:
                    dve.wait_ge(a_exp.sem, a_exp.at(s))
                    dve.reciprocal(flat(rr[:, :, :]), flat(rs[:, s.par])).then_inc(d_rr.sem, 1)
                elif n in (1, 2):
                    dve.wait_ge(p_R.sem, p_R.at(s, n))
                    dve.wait_ge(a_o.sem, a_o.at(s))
                    half = ao[:, 2 * (n - 1):2 * n, :]
                    tt(half, half, M, ALU.mult).then_inc(d_ao.sem, 1)
                elif n == 3:
                    dve.wait_ge(p_wo.sem, p_wo.at(s))
                    dve.wait_ge(g_x1b.sem, g_x1b.at(s))
                    tt(x2[:, s.par], x1b[:, s.par], M, ALU.add).then_inc(d_z2.sem, 1)
                elif n == 4:
                    dve.wait_ge(a_x2T.sem, a_x2T.at(s))
                    tt(x2T[:, s.par, 1], M, x2T[:, s.par, 0].bitcast(F32), ALU.subtract).then_inc(d_x2T.sem, 1)

            def router(s, part):
                step = [ROUTER_SIGNALS[part]]

                def did(ins):
                    step[0] += 1
                    ins.then_inc(d_gate.sem, 1)
                    return step[0]

                def after(k):
                    dve.wait_ge(d_gate.sem, d_gate.at(s, k))

                v = sc[:, :, :].rearrange("p t (g e) -> p (t g) e", e=EG)

                def ranks(val, gt, eq, rank, n):
                    for t in range(NT):
                        vj = val[:, t, :].rearrange("p (a e) -> p a e", a=1).to_broadcast([P, n, n])
                        vi = val[:, t, :].rearrange("p (e a) -> p e a", a=1).to_broadcast([P, n, n])
                        tt(gt[:, t], vj, vi, ALU.is_gt)
                        last = tt(eq[:, t], vj, vi, ALU.is_equal)
                    k = did(last)
                    after(k)
                    for t in range(NT):
                        last = tt(eq[:, t], eq[:, t], lower[:, 0:n, 0:n], ALU.mult)
                    after(did(last))
                    after(did(tt(gt.rearrange("p t i j -> p (t i j)"), gt.rearrange("p t i j -> p (t i j)"),
                                 eq.rearrange("p t i j -> p (t i j)"), ALU.add)))
                    did(dve.tensor_reduce(rank, gt.rearrange("p t i j -> p (t i) j"), AX.X, ALU.add))

                if part == 0:
                    dve.wait_ge(a_gate.sem, a_gate.at(s))
                    after(did(ts(flat(sc[:, :, :]), gth[:, :], 0.5, 0.5, ALU.mult, ALU.add)))
                    for n, (i, j) in enumerate([(0, 1), (0, 2), (0, 3), (1, 2), (1, 3), (2, 3)]):
                        last = tt(pair[:, :, n:n + 1], v[:, :, i:i + 1], v[:, :, j:j + 1], ALU.add)
                    after(did(last))
                    after(did(dve.tensor_reduce(gsum[:, :, :].rearrange("p t g -> p (t g)"), pair[:, :, :], AX.X, ALU.max)))
                    ranks(gsum, ggt[:, :, :, :], geq[:, :, :, :], grank[:, :, :].rearrange("p t g -> p (t g)"), GROUPS)
                elif part == 1:
                    after(step[0])
                    after(did(ts(gok[:, :, :], grank[:, :, :], float(TOPG) - 0.5, 2.0, ALU.is_lt, ALU.mult)))
                    m4 = msk[:, :, :].rearrange("p t (g e) -> p (t g) e", e=EG)
                    g4 = gok[:, :, :].rearrange("p t (g a) -> p (t g) a", a=1).to_broadcast([P, NT * GROUPS, EG])
                    after(did(tt(m4, v, g4, ALU.mult)))
                    ranks(msk, egt, eeq, erank[:, :, :].rearrange("p t e -> p (t e)"), E)
                else:
                    after(step[0])
                    for t in range(NT):
                        last = stt(wsel[:, t, :], erank[:, t, :], float(TOPK) - 0.5, sc[:, t, :], ALU.is_lt, ALU.mult,
                                   accum_out=wsum[:, t:t + 1])
                    last.then_inc(d_wsel.sem, 1)
                    dve.wait_ge(d_wsel.sem, d_wsel.at(s))
                    ts(wrec[:, :], wsum[:, :], 1e-6, None, ALU.add).then_inc(d_wsum.sem, 1)
                    dve.wait_ge(d_wsum.sem, d_wsum.at(s))
                    dve.reciprocal(wrec[:, :], wrec[:, :]).then_inc(d_wrec.sem, 1)
                    dve.wait_ge(d_wrec.sem, d_wrec.at(s))
                    for t in range(NT):
                        for n in range(2):
                            last = ts(comb[:, t, n, :], wsel[:, t, :], wrec[:, t:t + 1], None, ALU.mult)
                    last.then_inc(d_comb.sem, 1)
                assert step[0] == ROUTER_SIGNALS[part + 1], step[0]

            def hidden_gate(s, k):
                dve.wait_ge(a_tg.sem, a_tg.at(s, k + 1))
                t1 = flat(tg[:, :, :])
                stt(t1, t1, 1.0, bG[:, :], ALU.add, ALU.mult).then_inc(d_t1.sem, 1)

            def hidden_up(s, k):
                dve.wait_ge(d_t1.sem, d_t1.at(s, k + 1))
                dve.wait_ge(p_u.sem, p_u.at(s, k + 1))
                if k >= 2:
                    dve.wait_ge(p_y.sem, p_y.at(s, k - 1))
                elif not first(s):
                    dve.wait_ge(p_y.sem, p_y.at(s.plus(-1)))
                tt(flat(hid[:, k % 2]), flat(tg[:, :, :]), bU[:, :], ALU.mult).then_inc(d_t2.sem, 1)

            def hidden_combine(s, k):
                h = flat(hid[:, k % 2])
                dve.wait_ge(p_c.sem, p_c.at(s, k))
                dve.wait_ge(d_t2.sem, d_t2.at(s, k + 1))
                tt(h, h, bC[:, :], ALU.mult).then_inc(d_t3.sem, 1)

            def last_sum(s):
                dve.wait_ge(p_y.sem, p_y.at(s))
                if not (isinstance(s.l, int) and s.l < 2):
                    dve.wait_ge(s_out[s.par], 16 * s.half)
                stt(yo[:, s.par], cols(bY), 0.5, x2[:, s.par], ALU.mult, ALU.add).then_inc(d_z3.sem, 1)

            def body(s, A=False, B=False, T=False, C=False, F=False, mix_next=True):
                a, t, c, f = s.plus(1), s.plus(-1), s.plus(-2), s.plus(-3)
                for k in range(PAIRS + 1):
                    h = 2 * k
                    heads = B and h < HEADS
                    if heads:
                        clip(s, h)
                    if C and k < PAIRS:
                        hidden_gate(c, k)
                        hidden_up(c, k)
                    if C and k == 0:
                        dve.wait_ge(a_comb.sem, a_comb.at(c))
                        stt(combT[:, c.par, :], combh[:, :].bitcast(F32), minus_low[:, :], bM[0:2 * E, 0:TOK], ALU.mult, ALU.add).then_inc(d_combT.sem, 1)
                    if T and k == 0:
                        t_chunk(t, 0)
                    if T and k > 1 and k in TAIL_AT:
                        t_chunk(t, TAIL_AT.index(k))
                    if F and k == 0:
                        last_sum(f)
                    if heads:
                        clip(s, h + 1)
                    if C and 0 < k < PAIRS:
                        hidden_combine(c, k)
                    if F and k == 1:
                        dve.wait_ge(d_z3.sem, d_z3.at(f))
                        norm(2, f, yo[:, f.par], yo[:, f.par], d_yo)
                    if T and k == TAIL_AT[3]:
                        dve.wait_ge(d_z2.sem, d_z2.at(t))
                        norm(1, t, x2[:, t.par], x2[:, t.par], d_x2)
                    if T and k in ROUTER_AT:
                        router(t, ROUTER_AT.index(k))
                    if A and k < 8:
                        a_chunk(a, k)
                    if A and mix_next and k == MIX_AT:
                        mixes(a.plus(1))

            mixes(Step(0, 0))
            body(Step(0, -1), A=True)
            body(Step(0, 0), A=True, B=True)
            body(Step(0, 1), A=True, B=True, T=True)
            body(Step(0, 2), A=True, B=True, T=True, C=True)
            with dve.Fori(1, (L - 4) // 2) as i:
                body(Step(i, 1), A=True, B=True, T=True, C=True, F=True)
                body(Step(i, 2), A=True, B=True, T=True, C=True, F=True)
            body(Step((L - 4) // 2, 1), A=True, B=True, T=True, C=True, F=True)
            body(Step((L - 4) // 2, 2), A=True, B=True, T=True, C=True, F=True, mix_next=False)
            last_bodies(body)

        @block.gpsimd
        def _(pool):
            def rsqrt(n, s):
                pool.wait_ge(d_vpe[n].sem, d_vpe[n].at(s))
                pool.tensor_tensor(rstd[:, n, :], vpe[:, n, :], mhalf[:, :], ALU.pow).then_inc(g_rstd[n].sem, 1)

            def split_experts(w):
                for n in range(w * NWCH, (w + 1) * NWCH):
                    c = (n - w * NWCH) * WCH
                    pool.wait_ge(s_raw[n % 2], 16 * (n // 2 + 1))
                    pool.tensor_copy(W13[:, w, 0, :, c:c + WCH], wraw[:, n % 2]).then_inc(s_high, 1)
                    pool.wait_ge(s_high, n + 1)
                    pool.tensor_tensor(W13[:, w, 1, :, c:c + WCH], wraw[:, n % 2], W13[:, w, 0, :, c:c + WCH].bitcast(F32),
                                       ALU.subtract).then_inc(s_split, 1)

            def body(s, A=False, B=False, T=False, C=False, F=False):
                a, t, c, f = s.plus(1), s.plus(-1), s.plus(-2), s.plus(-3)
                if F:
                    rsqrt(2, f)
                if T:
                    rsqrt(1, t)
                if A:
                    rsqrt(0, a)
                    pool.wait_ge(d_x1.sem, d_x1.at(a))
                    if T:
                        pool.wait_ge(d_z2.sem, d_z2.at(t))
                    for n in range(NT):
                        last = pool.tensor_tensor(x1b[:, a.par, n, :], x1[:, n, :], bo_row[:, :], ALU.add)
                    last.then_inc(g_x1b.sem, 1)

            pool.wait_ge(s_zero, 1)
            pool.wait_ge(s_const, 16 * 9)
            body(Step(0, -1), A=True)
            split_experts(0)
            body(Step(0, 0), A=True, B=True)
            split_experts(1)
            body(Step(0, 1), A=True, B=True, T=True)
            body(Step(0, 2), A=True, B=True, T=True, C=True)
            with pool.Fori(1, (L - 2) // 2) as i:
                body(Step(i, 1), A=True, B=True, T=True, C=True, F=True)
                body(Step(i, 2), A=True, B=True, T=True, C=True, F=True)
            last_bodies(body)


def kernel(**inputs):
    import concourse.bacc as _bacc
    from concourse.bass_utils import run_bass_kernel_spmd as _run

    a = {k: np.asarray(v) for k, v in inputs.items()}
    at, xa, ff = "L0_attn_", "L0_xattn_", "L0_ffn_"

    def column(v):
        return v.reshape(ND, P).T

    def padded_rows(w):
        w = w.reshape(HEADS, HD, D)
        return np.concatenate([w, np.zeros_like(w)], axis=1).reshape(NHT, P, D)

    p = np.arange(P)
    arrays = {
        "x": a["x"],
        "xT": a["x"].transpose(0, 2, 1),
        "ctxT": a["ctx_768"].transpose(0, 2, 1),
        "vecs": np.stack([column(a[at + "mu_k"]), column(a[at + "mu_v"]), column(a[at + "mu_r"]), column(a[at + "w"]),
                          column(a[at + "u"]), column(a[xa + "bq"]), column(a[xa + "bk"])], axis=1),
        "rows": np.stack([np.broadcast_to(a[xa + "bv"], (P, D)), np.broadcast_to(a[xa + "bo"], (P, D))]),
        "wproj": np.stack([a[at + "Wk"].T, a[at + "Wv"].T, a[at + "Wr"].T, a[at + "W_out"].T, a[xa + "Wq"]]),
        "wctx": np.stack([a[xa + "Wk"], a[xa + "Wv"]]),
        "wo": padded_rows(a[xa + "Wo"]),
        "w1": np.concatenate([a[ff + "w1_s"], a[ff + "w1_e"].reshape(E * F, D)]).T,
        "w3": np.concatenate([a[ff + "w3_s"], a[ff + "w3_e"].reshape(E * F, D)]).T,
        "w2": np.concatenate([a[ff + "w2_s"].T.reshape(2, P, D), a[ff + "w2_e"].transpose(0, 2, 1)]),
        "wg": a[ff + "w_gate"].T,
        "ident": np.eye(P, dtype=np.float32),
        "sel": (np.arange(HEADS)[:, None, None] == HT * np.arange(NHT)[None, :, None] + p[None, None, :] // HB).astype(np.float32),
        "sel2": np.concatenate([np.concatenate([np.eye(E), np.zeros((E, 1))], 1), np.concatenate([np.eye(E), np.ones((E, 1))], 1)]).astype(np.float32),
        "parity": np.stack([p // HD % 2 == 0, p // HD % 2 == 1], axis=1).astype(np.float32),
        "below": np.ascontiguousarray(np.broadcast_to(np.tril(np.ones((E, E), np.float32), -1), (P, E, E))),
    }
    nc = _bacc.Bacc("TRN2", target_bir_lowering=False, num_devices=1)
    args = []
    for name, v in arrays.items():
        arrays[name] = v = np.ascontiguousarray(v)
        args.append(nc.dram_tensor(name, v.shape, mybir.dt.from_np(v.dtype), kind="ExternalInput").ap())
    out = nc.dram_tensor("out", (L, TOK, D), F32, kind="ExternalOutput").ap()
    decoder_layer(nc, *args, out)
    return _run(nc, [arrays], core_ids=[0]).results[0]["out"]
```

```python
from contextlib import ExitStack

import numpy as np

import concourse.bass as bass
from concourse import mybir

F32 = mybir.dt.float32
F32R = mybir.dt.float32r
ACT = mybir.ActivationFunctionType
ALU = mybir.AluOpType
AX = mybir.AxisListType

P = 128
L, TOK, D = 16, 256, 256
CKV = 192
CP = CKV // 2
NT = TOK // P
ND = D // P
HEADS, HD = 16, 16
HG = P // HD
E, F = 16, 128
GROUPS, TOPG, TOPK = 4, 2, 4
EG = E // GROUPS
PAIRS = E // 2 + 1
SCALE = float(HD) ** -0.5
CLAMP = 10000.0
EPS = 1e-5
SBUFS = 3
HB = 2 * HD
WCH = 256
NWCH = 2 * PAIRS * F // WCH
SPLIT_BY = [0, 4, 11, 13, 17, 2 * NWCH]


class Step:

    def __init__(self, i, off):
        self.i, self.off = i, off
        self.l = 2 * i + off
        self.half = i + off // 2
        self.par = off % 2

    def plus(self, k):
        return Step(self.i, self.off + k)


class Event:

    def __init__(self, sem, per):
        self.sem, self.per = sem, per

    def at(self, step, k=None):
        return step.l * self.per + (self.per if k is None else k)


def first(step):
    return isinstance(step.l, int) and step.l == 0


TAIL_AT = [1, 2, 4, 5, 6]
ROUTER_AT = [6, 7, 8]
ROUTER_SIGNALS = [0, 7, 13, 13]

VECS = ["mu_k", "mu_v", "mu_r", "w", "u", "bq", "bk"]


def decoder_layer(nc, x, xT, ctxT, vecs, rows, wproj, wctx, wo, w1, w3, w2, wg, ident, sel, sel2, picks, below, out):
    with ExitStack() as ctx:
        def sb(name, shape, dt=F32):
            return ctx.enter_context(nc.sbuf_tensor(name, shape, dt))

        def bank(name):
            return ctx.enter_context(nc.psum_tensor(name, [P, 512], F32))

        def sem(name):
            return ctx.enter_context(nc.semaphore(name))

        def event(name, per=1):
            return Event(sem(name), per)

        Wp = sb("Wp", [P, 5, ND, D])
        WK, WV, WR, WOUT, WQ = range(5)
        Wo = sb("Wo", [P, ND, D])
        Wc = sb("Wc", [CP, 2, 2, 2, D], F32R)
        W13 = sb("W13", [P, 2, 2, ND, 2 * PAIRS * F], F32R)
        late = sb("late", [P, 2 * ND * WCH])
        wraw = late[:, :].rearrange("p (r j c) -> p r j c", r=2, j=ND)
        W2 = sb("W2", [P, 2 * PAIRS, D])
        Wg = sb("Wg", [P, ND, E])
        Wgs = sb("Wgs", [P, 2, ND, E], F32R)
        idn = sb("idn", [P, P])
        selh = sb("selh", [2 * HEADS, ND, P], F32R)
        sele_raw = sb("sele_raw", [2 * E, E + 1])
        sele = sb("sele", [2 * E, E], F32R)
        pick = sb("pick", [P, 2, 2, P], F32R)
        lower = sb("lower", [P, E, E])
        vec = sb("vec", [P, len(VECS), ND])
        minus_low = sb("minus_low", [2 * E, 1])
        bv_row = sb("bv_row", [P, D])
        bo_row = sb("bo_row", [P, D])
        decay = sb("decay", [P, ND])
        ew = sb("ew", [P, ND])
        eu = sb("eu", [P, ND])
        qb = sb("qb", [P, ND])
        mhalf = sb("mhalf", [P, NT])

        xTs = sb("xTs", [P, 2, ND, TOK])
        xs = sb("xs", [P, NT, D])
        mix = sb("mix", [P, 3, ND, TOK])
        cTs = sb("cTs", [CP, 2, 2, TOK], F32R)
        dx = mix[:, 2]
        ek = sb("ek", [P, ND, TOK])
        ekv = sb("ekv", [P, ND, TOK])
        thr = sb("thr", [P, ND, TOK])
        den = sb("den", [P, ND, TOK])
        cT = den[0:CP]
        num = sb("num", [P, ND, TOK])
        Sd = sb("Sd", [P, ND, TOK])
        Sn = sb("Sn", [P, ND, TOK])
        x1 = sb("x1", [P, NT, D])
        x1T = thr
        x1b = sb("x1b", [P, 2, NT, D])
        QT = sb("QT", [P, 2, ND, TOK], F32R)
        KT = sb("KT", [P, 2, ND, TOK], F32R)
        Vs = sb("Vs", [P, 2, NT, HEADS // 2, 3, HD])

        QK = sb("QK", [P, 2, 2, TOK], F32R)
        Sc = sb("Sc", [P, SBUFS, NT, TOK])
        nmx = sb("nmx", [P, HEADS, NT])
        rs = sb("rs", [P, 2, NT, HEADS])
        rr = sb("rr", [P, NT, 2, HEADS])
        PT = sb("PT", [P, 2, NT, TOK])
        wc_raw = PT[0:CP]
        rT = sb("rT", [2 * HEADS, TOK], F32R)
        ao = sb("ao", [P, ND, TOK])
        gth = sb("gth", [P, NT * E])
        sc = sb("sc", [P, NT, E])
        pair = sb("pair", [P, NT * GROUPS, 6])
        gsum = sb("gsum", [P, NT, GROUPS])
        ggt = sb("ggt", [P, NT, GROUPS, GROUPS])
        geq = sb("geq", [P, NT, GROUPS, GROUPS])
        grank = sb("grank", [P, NT, GROUPS])
        gok = sb("gok", [P, NT, GROUPS])
        msk = sb("msk", [P, NT, E])
        egt = num[:, :, :].rearrange("p t (i j) -> p t i j", i=E)
        eeq = den[:, :, :].rearrange("p t (i j) -> p t i j", i=E)
        erank = sb("erank", [P, NT, E])
        wsel = sb("wsel", [P, NT, E])
        wsum = sb("wsum", [P, NT])
        wrec = sb("wrec", [P, NT])
        x2 = sb("x2", [P, 2, NT, D])
        x2T = sb("x2T", [P, 2, 2, ND, TOK], F32R)
        comb = sb("comb", [P, NT, 2, E])
        combT = sb("combT", [2 * E, TOK], F32R)

        yo = late[:, 0:NT * D].rearrange("p (t d) -> p t d", t=NT)
        tg = late[:, NT * D:].rearrange("p (i t) -> p i t", i=2)
        hid = sb("hid", [P, 2, 2, TOK])

        st = sb("st", [P, 3, NT, 6])
        mv = sb("mv", [P, 3, NT, 2])
        vpe = sb("vpe", [P, 3, NT])
        rstd = sb("rstd", [P, 3, NT])

        bG, bU, bC, bY, bS, bT, bO, bM = (bank(n) for n in ("bG", "bU", "bC", "bY", "bS", "bT", "bO", "bM"))

        def cols(b, n=2):
            return b[:, :].rearrange("p (n c) -> p n c", n=n)

        s_att = sem("s_att")
        s_w2 = sem("s_w2")
        s_raw = [sem("s_raw0"), sem("s_raw1")]
        s_high = sem("s_high")
        s_split = sem("s_split")
        s_small = sem("s_small")
        s_vec = sem("s_vec")
        s_wk = sem("s_wk")
        s_const = sem("s_const")
        s_zero = sem("s_zero")
        s_ew = sem("s_ew")
        s_decay = sem("s_decay")
        s_pick = sem("s_pick")
        s_picked = sem("s_picked")
        s_wc = sem("s_wc")
        s_qb = sem("s_qb")
        s_xT = [sem("s_xT0"), sem("s_xT1")]
        s_x = sem("s_x")
        s_ctx = sem("s_ctx")
        s_out = sem("s_out")
        g_dx = event("g_dx")
        g_dmix = event("g_dmix", 3)
        g_mix = event("g_mix", 3)
        p_kvr = event("p_kvr", 3)
        a_ek = event("a_ek")
        d_ekv = event("d_ekv")
        a_thr = event("a_thr")
        g_den = event("g_den", 4)
        g_state = event("g_state", 4)
        d_rden = event("d_rden", 2)
        d_num = event("d_num")
        d_wkv = event("d_wkv")
        p_wout = event("p_wout")
        d_z1 = event("d_z1")
        d_x1 = event("d_x1")
        g_x1b = event("g_x1b")
        p_x1T = event("p_x1T")
        a_x1T = event("a_x1T")
        p_q = event("p_q")
        a_ctx = event("a_ctx")
        g_ctx = event("g_ctx")
        a_q = event("a_q")
        d_q = event("d_q")
        p_k = event("p_k")
        a_k = event("a_k")
        d_k = event("d_k")
        p_v = event("p_v")
        d_v = event("d_v")
        d_st = [event(f"d_st{n}") for n in range(3)]
        d_mv = [event(f"d_mv{n}") for n in range(3)]
        d_vpe = [event(f"d_vpe{n}") for n in range(3)]
        g_rstd = [event(f"g_rstd{n}") for n in range(3)]
        p_stack = event("p_stack", HEADS // 2)
        a_stack = event("a_stack", HEADS // 2)
        p_s = event("p_s", HEADS)
        d_clip = event("d_clip", HEADS)
        d_max = event("d_max", HEADS)
        a_exp = event("a_exp", HEADS)
        p_t = event("p_t", HEADS)
        a_pt = event("a_pt", HEADS)
        p_av = event("p_av", HEADS)
        a_o = event("a_o")
        d_rr = event("d_rr")
        p_rT = event("p_rT")
        a_rT = event("a_rT")
        d_rT = event("d_rT")
        p_R = event("p_R")
        d_ao = event("d_ao")
        p_wo = event("p_wo")
        d_z2 = event("d_z2")
        d_x2 = event("d_x2")
        p_x2T = event("p_x2T")
        a_x2T = event("a_x2T")
        d_x2T = event("d_x2T")
        p_gate = event("p_gate")
        a_gate = event("a_gate")
        d_gate = event("d_gate", ROUTER_SIGNALS[-1])
        d_wsel = event("d_wsel")
        d_wsum = event("d_wsum")
        d_wrec = event("d_wrec")
        d_comb = event("d_comb")
        p_comb = event("p_comb")
        a_comb = event("a_comb")
        d_combT = event("d_combT")
        p_g = event("p_g", PAIRS)
        p_u = event("p_u", PAIRS)
        p_c = event("p_c", PAIRS - 1)
        a_tg = event("a_tg", PAIRS)
        d_t1 = event("d_t1", PAIRS)
        d_t2 = event("d_t2", PAIRS)
        d_t3 = event("d_t3", PAIRS - 1)
        p_y = event("p_y", PAIRS)
        d_z3 = event("d_z3")
        d_yo = event("d_yo")

        block = ctx.enter_context(nc.Block())

        def last_bodies(body):
            body(Step(L // 2, -1), B=True, T=True, C=True, F=True)
            body(Step(L // 2, 0), T=True, C=True, F=True)
            body(Step(L // 2, 1), C=True, F=True)
            body(Step(L // 2, 2), F=True)

        def bodies(eng, body):
            body(Step(0, -1), A=True)
            body(Step(0, 0), A=True, B=True)
            body(Step(0, 1), A=True, B=True, T=True)
            body(Step(0, 2), A=True, B=True, T=True, C=True)
            with eng.Fori(1, (L - 2) // 2) as i:
                body(Step(i, 1), A=True, B=True, T=True, C=True, F=True)
                body(Step(i, 2), A=True, B=True, T=True, C=True, F=True)
            last_bodies(body)

        @block.sync
        def _(sp):
            def load_turned(step):
                p = step.par
                if not first(step):
                    sp.wait_ge(g_mix.sem, g_mix.at(step.plus(-1)))
                sp.dma_start(xTs[:, p], xT[bass.ds(step.l, 1)].rearrange("a (j p) t -> p (a j) t", p=P)).then_inc(s_xT[p], 16)

            def load(step):
                if not first(step):
                    sp.wait_ge(d_z1.sem, d_z1.at(step.plus(-1)))
                sp.dma_start(xs[:, :, :], x[bass.ds(step.l, 1)].rearrange("a (t p) d -> p (a t) d", p=P)).then_inc(s_x, 16)
                if not (isinstance(step.l, int) and step.l < 3):
                    sp.wait_ge(d_wsel.sem, d_wsel.at(step.plus(-3)))
                elif not first(step):
                    sp.wait_ge(d_wkv.sem, d_wkv.at(step.plus(-1)))
                sp.dma_start(cT, ctxT[bass.ds(step.l, 1)].rearrange("a (j p) t -> p (a j) t", p=CP)).then_inc(s_ctx, 16)

            sp.dma_start(vec[:, :, :], vecs).then_inc(s_vec, 16)
            load_turned(Step(0, 0))
            sp.dma_start(Wp[:, WK], wproj[WK].rearrange("(j p) d -> p j d", p=P)).then_inc(s_wk, 16)
            sp.dma_start(Wp[:, WV:], wproj[WV:].rearrange("w (j p) d -> p w j d", p=P)).then_inc(s_att, 16)
            load(Step(0, 0))
            sp.dma_start(wc_raw, wctx.rearrange("w (j p) d -> p w j d", p=CP)).then_inc(s_att, 16)
            sp.dma_start(idn[:, :], ident).then_inc(s_const, 16)
            sp.dma_start(bv_row[:, :], rows[0]).then_inc(s_const, 16)
            sp.dma_start(bo_row[:, :], rows[1]).then_inc(s_const, 16)
            sp.dma_start(Sc[0:2 * HEADS, 1, 0], sel.rearrange("h n c -> h (n c)")).then_inc(s_pick, 16)
            sp.dma_start(sele_raw[:, :], sel2).then_inc(s_const, 16)
            sp.dma_start(lower[:, :, :], below).then_inc(s_const, 16)
            sp.dma_start(Wg[:, :, :], wg.rearrange("(j p) e -> p j e", p=P)).then_inc(s_const, 16)
            sp.dma_start(Wo[:, :, :], wo.rearrange("(j p) h -> p j h", p=P)).then_inc(s_att, 16)
            sp.dma_start(Sc[:, 0].rearrange("p t (n f) -> p (t n) f", f=P), picks.rearrange("n p f -> p n f")).then_inc(s_pick, 16)

            def body(s, A=False, B=False, T=False, C=False, F=False):
                a, f = s.plus(1), s.plus(-3)
                if F:
                    sp.wait_ge(d_yo.sem, d_yo.at(f))
                    sp.dma_start(out[bass.ds(f.l, 1)].rearrange("a (t p) d -> p (a t) d", p=P), yo[:, :, :]).then_inc(s_out, 16)
                if A and not (isinstance(a.l, int) and a.l == L - 1):
                    load_turned(a.plus(1))
                    load(a.plus(1))

            def load_experts(until):
                for n in range(SPLIT_BY[SPLIT_BY.index(until) - 1], until):
                    src = w3 if n >= NWCH else w1
                    if n >= 2:
                        sp.wait_ge(s_split, n - 1)
                    c = n % NWCH * WCH
                    sp.dma_start(wraw[:, n % 2], src[:, c:c + WCH].rearrange("(j p) f -> p j f", p=P)).then_inc(s_raw[n % 2], 16)

            load_turned(Step(0, 1))
            load_experts(SPLIT_BY[1])
            load(Step(0, 1))
            load_experts(SPLIT_BY[2])
            load_experts(SPLIT_BY[3])
            load_turned(Step(0, 2))
            load(Step(0, 2))
            load_experts(SPLIT_BY[4])
            load_turned(Step(0, 3))
            load_experts(SPLIT_BY[5])
            sp.dma_start(W2[:, :, :], w2.rearrange("c p h -> p c h")).then_inc(s_w2, 16)
            load(Step(0, 3))
            body(Step(0, 2), A=True, B=True, T=True, C=True)
            with sp.Fori(1, (L - 4) // 2) as i:
                body(Step(i, 1), A=True, B=True, T=True, C=True, F=True)
                body(Step(i, 2), A=True, B=True, T=True, C=True, F=True)
            body(Step((L - 4) // 2, 1), A=True, B=True, T=True, C=True, F=True)
            body(Step((L - 4) // 2, 2), A=True, B=True, T=True, C=True, F=True)
            last_bodies(body)
            sp.wait_ge(s_out, 16 * L)

        @block.tensor
        def _(pe):
            mm = pe.matmul

            def proj(dst, w, src, n):
                for m in range(ND):
                    for j in range(n):
                        last = mm(dst[:, m, :], w[:, j, m * P:(m + 1) * P], src[:, j, :], start=(j == 0), stop=(j == n - 1))
                return last

            def token_proj(dst, w, src, n):
                for t in range(NT):
                    for j in range(n):
                        last = mm(dst[:, t, :], src[:, j, t * P:(t + 1) * P], w[:, j, :], start=(j == 0), stop=(j == n - 1))
                return last

            def turn(dst, src):
                for j in range(ND):
                    for t in range(NT):
                        last = pe.transpose(dst[:, j, t * P:(t + 1) * P], src[:, t, j * P:(j + 1) * P], idn[:, :])
                return last

            M = cols(bM)

            def split(dst, w, x, js, start=True, stop=True):
                terms = [(j, a, b) for j in js for a, b in ((0, 0), (0, 1), (1, 0))]
                for n, (j, a, b) in enumerate(terms):
                    last = mm(dst, w(a, j), x(b, j), start=(start and n == 0), stop=(stop and n == len(terms) - 1))
                return last

            def a_chunk(s, n, t, c):
                if n == 0:
                    if first(s):
                        pe.wait_ge(s_wk, 16)
                    elif c is not None:
                        pe.wait_ge(d_combT.sem, d_combT.at(c))
                    else:
                        pe.wait_ge(d_k.sem, d_k.at(s.plus(-1)))
                    pe.wait_ge(g_mix.sem, g_mix.at(s, 1))
                    proj(M, Wp[:, WK], mix[:, 0], ND).then_inc(p_kvr.sem, 1)
                elif n == 1:
                    if first(s):
                        pe.wait_ge(s_att, 48)
                    pe.wait_ge(g_mix.sem, g_mix.at(s, 2))
                    pe.wait_ge(a_ek.sem, a_ek.at(s))
                    if t is not None:
                        pe.wait_ge(d_rT.sem, d_rT.at(t))
                    proj(M, Wp[:, WV], mix[:, 1], ND).then_inc(p_kvr.sem, 1)
                elif n == 2:
                    pe.wait_ge(g_mix.sem, g_mix.at(s, 3))
                    pe.wait_ge(d_ekv.sem, d_ekv.at(s))
                    if t is not None:
                        pe.wait_ge(d_ao.sem, d_ao.at(t))
                    proj(M, Wp[:, WR], mix[:, 2], ND).then_inc(p_kvr.sem, 1)
                elif n == 8:
                    pe.wait_ge(d_q.sem, d_q.at(s))
                    for m in range(ND):
                        last = split(M[:, m, :], lambda a, j: Wc[:, 0, a, j, m * P:(m + 1) * P], lambda b, j: cTs[:, b, j, :], range(2))
                    last.then_inc(p_k.sem, 1)
                elif n == 4:
                    if first(s):
                        pe.wait_ge(s_wc, 2)
                    pe.wait_ge(g_ctx.sem, g_ctx.at(s))
                    pe.wait_ge(a_thr.sem, a_thr.at(s))
                    if t is not None:
                        pe.wait_ge(d_z2.sem, d_z2.at(t))
                    for i in range(NT):
                        last = split(M[:, i, :], lambda a, j: cTs[:, a, j, i * P:(i + 1) * P], lambda b, j: Wc[:, 1, b, j, :], range(2))
                    last.then_inc(p_v.sem, 1)
                elif n == 5:
                    pe.wait_ge(d_v.sem, d_v.at(s))
                    if t is not None:
                        pe.wait_ge(d_x2T.sem, d_x2T.at(t))
                    pe.wait_ge(d_wkv.sem, d_wkv.at(s))
                    token_proj(M, Wp[:, WOUT], num, ND).then_inc(p_wout.sem, 1)
                elif n == 6:
                    if first(s):
                        pe.wait_ge(s_const, 16 * 6)
                    pe.wait_ge(d_x1.sem, d_x1.at(s))
                    if t is not None:
                        pe.wait_ge(a_gate.sem, a_gate.at(t))
                    turn(M, x1).then_inc(p_x1T.sem, 1)
                elif n == 7:
                    if first(s):
                        pe.wait_ge(s_qb, 2)
                    pe.wait_ge(a_x1T.sem, a_x1T.at(s))
                    proj(M, Wp[:, WQ], x1T, ND).then_inc(p_q.sem, 1)

            def t_chunk(s, n, a):
                if n == 0:
                    if a is not None:
                        pe.wait_ge(a_ek.sem, a_ek.at(a))
                    else:
                        pe.wait_ge(d_combT.sem, d_combT.at(s.plus(-1)))
                    pe.wait_ge(d_rr.sem, d_rr.at(s))
                    for t in range(NT):
                        last = pe.transpose(bM[0:2 * HEADS, t * P:(t + 1) * P], rr[:, t].rearrange("p a h -> p (a h)"), idn[:, :])
                    last.then_inc(p_rT.sem, 1)
                elif n == 1:
                    pe.wait_ge(d_rT.sem, d_rT.at(s))
                    if a is not None:
                        pe.wait_ge(d_ekv.sem, d_ekv.at(a))
                    for i in range(ND):
                        last = mm(M[:, i, :], selh[:, i, :], rT[:, :], start=True, stop=True)
                    last.then_inc(p_R.sem, 1)
                elif n == 2:
                    if a is not None:
                        pe.wait_ge(a_thr.sem, a_thr.at(a))
                    pe.wait_ge(d_ao.sem, d_ao.at(s))
                    token_proj(M, Wo, ao, ND).then_inc(p_wo.sem, 1)
                elif n == 3:
                    if a is not None:
                        pe.wait_ge(d_v.sem, d_v.at(a))
                    pe.wait_ge(d_x2.sem, d_x2.at(s))
                    turn(M, x2[:, s.par]).then_inc(p_x2T.sem, 1)
                elif n == 4:
                    if a is not None:
                        pe.wait_ge(d_z1.sem, d_z1.at(a))
                    pe.wait_ge(d_x2T.sem, d_x2T.at(s))
                    for t in range(NT):
                        last = split(bM[:, t * E:(t + 1) * E], lambda a, j: x2T[:, s.par, a, j, t * P:(t + 1) * P],
                                     lambda b, j: Wgs[:, b, j, :], range(ND))
                    last.then_inc(p_gate.sem, 1)

            def turn_combine(s, a):
                if a is not None:
                    pe.wait_ge(d_k.sem, d_k.at(a))
                else:
                    pe.wait_ge(a_gate.sem, a_gate.at(s))
                pe.wait_ge(d_comb.sem, d_comb.at(s))
                for t in range(NT):
                    last = pe.transpose(bM[0:2 * E, t * P:(t + 1) * P], comb[:, t].rearrange("p a e -> p (a e)"), idn[:, :])
                last.then_inc(p_comb.sem, 1)

            def stack(s, g, c):
                if g == 0:
                    pe.wait_ge(d_q.sem, d_q.at(s))
                    pe.wait_ge(d_k.sem, d_k.at(s))
                    if first(s):
                        pe.wait_ge(s_picked, 2)
                    else:
                        pe.wait_ge(a_stack.sem, a_stack.at(s.plus(-1)))
                else:
                    pe.wait_ge(a_stack.sem, a_stack.at(s, g))
                if c is not None:
                    pe.wait_ge(d_t3.sem, d_t3.at(*c))
                j, r = g // 4, 32 * (g % 4)
                for n, parts in enumerate((QT, KT)):
                    for b in range(2):
                        last = mm(cols(bC)[:, n, :], pick[r:r + 32, n, b, :], parts[r:r + 32, b, j, :], start=(b == 0), stop=(b == 1))
                last.then_inc(p_stack.sem, 1)

            def scores(s, h, two):
                g, m = divmod(h, 2)
                if m == 0:
                    pe.wait_ge(a_stack.sem, a_stack.at(s, g + 1))
                if h >= (2 if two else 1):
                    pe.wait_ge(d_clip.sem, d_clip.at(s, h - 1 if two else h))
                elif not first(s):
                    pe.wait_ge(d_clip.sem, d_clip.at(s.plus(-1)))
                r = 64 * m
                for t in range(NT):
                    last = mm(cols(bG if two and m else bS)[:, t, :], QK[r:r + 64, g % 2, 0, t * P:(t + 1) * P], QK[r:r + 64, g % 2, 1, :], start=True, stop=True)
                last.then_inc(p_s.sem, 1)

            def turn_probs(s, h):
                pe.wait_ge(a_exp.sem, a_exp.at(s, h + 1))
                if h:
                    pe.wait_ge(a_pt.sem, a_pt.at(s, h))
                turn(cols(bT), Sc[:, h % SBUFS]).then_inc(p_t.sem, 1)

            def values(s, h):
                pe.wait_ge(a_pt.sem, a_pt.at(s, h + 1))
                if h == 0:
                    pe.wait_ge(d_v.sem, d_v.at(s))
                    if not first(s):
                        pe.wait_ge(a_o.sem, a_o.at(s.plus(-1)))
                g, m = divmod(h, 2)
                i, c = divmod(g, P // HB)
                for k in range(NT):
                    v = Vs[:, s.par, k, g].rearrange("p b f -> p (b f)")[:, m * HD:m * HD + HB]
                    last = mm(cols(bO)[HB * c:HB * (c + 1), i, :], v, PT[:, h % 2, k, :],
                              start=(m == 0 and k == 0), stop=(m == 1 and k == NT - 1))
                last.then_inc(p_av.sem, 1)

            def gate(s, k):
                if k == 0:
                    pe.wait_ge(d_x2T.sem, d_x2T.at(s))
                    if first(s):
                        pe.wait_ge(d_clip.sem, d_clip.at(s.plus(1)))
                    else:
                        pe.wait_ge(d_t1.sem, d_t1.at(s.plus(-1)))
                else:
                    pe.wait_ge(d_t1.sem, d_t1.at(s, k))
                for i in range(2):
                    c = (2 * k + i) * F
                    last = split(cols(bG)[:, i, :], lambda a, j: W13[:, 0, a, j, c:c + F], lambda b, j: x2T[:, s.par, b, j, :], range(ND))
                last.then_inc(p_g.sem, 1)

            def up(s, k):
                if k:
                    pe.wait_ge(d_t2.sem, d_t2.at(s, k))
                elif not first(s):
                    pe.wait_ge(d_t2.sem, d_t2.at(s.plus(-1)))
                for i in range(2):
                    c = (2 * k + i) * F
                    last = split(cols(bU)[:, i, :], lambda a, j: W13[:, 1, a, j, c:c + F], lambda b, j: x2T[:, s.par, b, j, :], range(ND))
                last.then_inc(p_u.sem, 1)

            def combine(s, k, b):
                if k == 1:
                    pe.wait_ge(d_combT.sem, d_combT.at(s))
                if b is not None and k < HEADS // 2 - 1:
                    pe.wait_ge(a_stack.sem, a_stack.at(b, k + 2))
                elif k > 1:
                    pe.wait_ge(d_t3.sem, d_t3.at(s, k - 1))
                elif not first(s):
                    pe.wait_ge(d_t3.sem, d_t3.at(s.plus(-1)))
                for i in range(2):
                    e = 2 * (k - 1) + i
                    last = mm(cols(bC)[:, i, :], sele[:, e:e + 1].to_broadcast([2 * E, P]), combT[:, :], start=True, stop=True)
                last.then_inc(p_c.sem, 1)

            def down(s, k):
                if k == 0:
                    pe.wait_ge(d_t2.sem, d_t2.at(s, 1))
                    if not first(s):
                        pe.wait_ge(d_z3.sem, d_z3.at(s.plus(-1)))
                else:
                    pe.wait_ge(d_t3.sem, d_t3.at(s, k))
                for t in range(NT):
                    for c in range(2):
                        last = mm(cols(bY)[:, t, :], hid[:, k % 2, c, t * P:(t + 1) * P], W2[:, 2 * k + c, :],
                                  start=(k == 0 and t == 0 and c == 0), stop=(k == PAIRS - 1 and c == 1), skip_group_check=True)
                last.then_inc(p_y.sem, 1)

            def body(s, A=False, B=False, T=False, C=False, F=False):
                a, t, c, f = s.plus(1), s.plus(-1), s.plus(-2), s.plus(-3)
                for k in range(PAIRS + 1):
                    h = 2 * k
                    heads = B and h < HEADS
                    if heads and k:
                        scores(s, h, not C)
                    if C and k < PAIRS:
                        gate(c, k)
                    if heads and not k:
                        scores(s, h, not C)
                    if B and k < HEADS // 2 - 1:
                        stack(s, k + 1, (c, k - 1) if C and k > 1 else None)
                    if heads and not C:
                        scores(s, h + 1, not C)
                    if B and 0 < h <= HEADS:
                        turn_probs(s, h - 1)
                    if C and k < PAIRS:
                        up(c, k)
                    if C and k == 0:
                        turn_combine(c, s if B else None)
                    if T and k in TAIL_AT:
                        t_chunk(t, TAIL_AT.index(k), a if A else None)
                    if A and k == 8:
                        a_chunk(a, k, t if T else None, c if C else None)
                    if B and 0 < h <= HEADS:
                        values(s, h - 1)
                    if heads and C:
                        scores(s, h + 1, not C)
                    if C and 0 < k < PAIRS:
                        combine(c, k, s if B else None)
                    if heads:
                        turn_probs(s, h)
                    if C and k:
                        down(c, k - 1)
                    if A and k == PAIRS:
                        stack(a, 0, (c, PAIRS - 1) if C else None)
                    if A and k < 8:
                        a_chunk(a, k, t if T else None, c if C else None)
                    if heads:
                        values(s, h)

            pe.wait_ge(s_zero, 1)
            body(Step(0, -1), A=True)
            body(Step(0, 0), A=True, B=True)
            pe.wait_ge(s_small, 4)
            body(Step(0, 1), A=True, B=True, T=True)
            pe.wait_ge(s_w2, 16)
            pe.wait_ge(s_split, 2 * NWCH)
            body(Step(0, 2), A=True, B=True, T=True, C=True)
            with pe.Fori(1, (L - 2) // 2) as i:
                body(Step(i, 1), A=True, B=True, T=True, C=True, F=True)
                body(Step(i, 2), A=True, B=True, T=True, C=True, F=True)
            last_bodies(body)

        @block.scalar
        def _(act):
            fn = act.activation
            M = bM[:, :]

            def flat(t):
                return t.rearrange("p a b -> p (a b)")

            act.wait_ge(s_vec, 16)
            fn(ew[:, :], vec[:, 3, :], ACT.Exp).then_inc(s_ew, 1)
            fn(eu[:, :], vec[:, 4, :], ACT.Exp)
            act.wait_ge(s_ew, 1)
            fn(decay[:, :], ew[:, :], ACT.Exp, scale=-1.0).then_inc(s_decay, 1)
            act.wait_ge(s_qb, 2)

            def a_chunk(s, n):
                if n == 0:
                    act.wait_ge(p_kvr.sem, p_kvr.at(s, 1))
                    if not first(s):
                        act.wait_ge(g_state.sem, g_state.at(s.plus(-1)))
                        act.wait_ge(p_k.sem, p_k.at(s.plus(-1)))
                    fn(flat(ek[:, :, :]), M, ACT.Exp).then_inc(a_ek.sem, 1)
                    act.wait_ge(s_ctx, 16 * (s.l + 1))
                    fn(flat(cTs[:, 0]), flat(cT), ACT.Copy).then_inc(a_ctx.sem, 1)
                elif n == 2:
                    act.wait_ge(p_kvr.sem, p_kvr.at(s, 3))
                    fn(flat(thr[:, :, :]), M, ACT.Tanh, scale=0.5).then_inc(a_thr.sem, 1)
                elif n == 8:
                    act.wait_ge(p_k.sem, p_k.at(s))
                    if not first(s):
                        act.wait_ge(p_stack.sem, p_stack.at(s.plus(-1)))
                    for j in range(ND):
                        last = fn(KT[:, 0, j, :], cols(bM)[:, j, :], ACT.Identity, bias=vec[:, 6, j:j + 1])
                    last.then_inc(a_k.sem, 1)
                elif n == 6:
                    act.wait_ge(p_x1T.sem, p_x1T.at(s))
                    fn(flat(x1T[:, :, :]), M, ACT.Copy).then_inc(a_x1T.sem, 1)
                elif n == 7:
                    act.wait_ge(p_q.sem, p_q.at(s))
                    if not first(s):
                        act.wait_ge(p_stack.sem, p_stack.at(s.plus(-1)))
                    for j in range(ND):
                        last = fn(QT[:, 0, j, :], cols(bM)[:, j, :], ACT.Identity, bias=qb[:, j:j + 1])
                    last.then_inc(a_q.sem, 1)

            def copy_stack(s, g):
                act.wait_ge(p_stack.sem, p_stack.at(s, g + 1))
                if g >= 2:
                    act.wait_ge(p_s.sem, p_s.at(s, 2 * g - 2))
                elif not first(s):
                    act.wait_ge(p_s.sem, p_s.at(s.plus(-1), HEADS - 2 + 2 * g))
                fn(QK[:, g % 2].rearrange("p n t -> p (n t)"), bC[:, :], ACT.Copy).then_inc(a_stack.sem, 1)

            def exps(s, h):
                act.wait_ge(d_max.sem, d_max.at(s, h + 1))
                for t in range(NT):
                    last = fn(Sc[:, h % SBUFS, t, :], Sc[:, h % SBUFS, t, :], ACT.Exp, bias=nmx[:, h, t:t + 1], accum_out=rs[:, s.par, t, h:h + 1])
                last.then_inc(a_exp.sem, 1)

            def copy_probs(s, h):
                act.wait_ge(p_t.sem, p_t.at(s, h + 1))
                if first(s) and h == 0:
                    act.wait_ge(s_wc, 2)
                if h >= 2:
                    act.wait_ge(p_av.sem, p_av.at(s, h - 1))
                fn(flat(PT[:, h % 2]), bT[:, :], ACT.Copy).then_inc(a_pt.sem, 1)

            def copy_out(s):
                act.wait_ge(p_av.sem, p_av.at(s))
                if not first(s):
                    act.wait_ge(p_wo.sem, p_wo.at(s.plus(-1)))
                fn(flat(ao[:, :, :]), bO[:, :], ACT.Copy).then_inc(a_o.sem, 1)

            def t_chunk(s, n):
                if n == 0:
                    act.wait_ge(p_rT.sem, p_rT.at(s))
                    fn(rT[:, :], bM[0:2 * HEADS, 0:TOK], ACT.Copy).then_inc(a_rT.sem, 1)
                elif n == 3:
                    act.wait_ge(p_x2T.sem, p_x2T.at(s))
                    fn(flat(x2T[:, s.par, 0]), M, ACT.Copy).then_inc(a_x2T.sem, 1)
                elif n == 4:
                    act.wait_ge(p_gate.sem, p_gate.at(s))
                    fn(gth[:, :], bM[:, 0:NT * E], ACT.Tanh, scale=0.5).then_inc(a_gate.sem, 1)

            def body(s, A=False, B=False, T=False, C=False, F=False):
                a, t, c, f = s.plus(1), s.plus(-1), s.plus(-2), s.plus(-3)
                for k in range(PAIRS + 1):
                    h = 2 * k
                    heads = B and h < HEADS
                    if C and k < PAIRS:
                        act.wait_ge(p_g.sem, p_g.at(c, k + 1))
                        if k:
                            act.wait_ge(d_t2.sem, d_t2.at(c, k))
                        elif not first(c):
                            act.wait_ge(d_t2.sem, d_t2.at(c.plus(-1)))
                        fn(flat(tg[:, :, :]), bG[:, :], ACT.Tanh, scale=0.5).then_inc(a_tg.sem, 1)
                    if B and k < HEADS // 2 - 1:
                        copy_stack(s, k + 1)
                    if A and k == PAIRS:
                        copy_stack(a, 0)
                    if heads and not C:
                        exps(s, h)
                    if B and 0 < h <= HEADS:
                        copy_probs(s, h - 1)
                    if heads and C:
                        exps(s, h)
                    if T and k in TAIL_AT:
                        t_chunk(t, TAIL_AT.index(k))
                    if B and h == HEADS:
                        copy_out(s)
                    if C and k == 0:
                        act.wait_ge(p_comb.sem, p_comb.at(c))
                        fn(combT[:, :], bM[0:2 * E, 0:TOK], ACT.Copy).then_inc(a_comb.sem, 1)
                    if heads and not C:
                        exps(s, h + 1)
                    if heads:
                        copy_probs(s, h)
                    if heads and C:
                        exps(s, h + 1)
                    if A and k < PAIRS:
                        a_chunk(a, k)

            bodies(act, body)

        @block.vector
        def _(dve):
            stt, tt, ts = dve.scalar_tensor_tensor, dve.tensor_tensor, dve.tensor_scalar
            M = cols(bM)

            def flat(t):
                return t.rearrange("p a b -> p (a b)")

            def moments(n, s, src):
                for t in range(NT):
                    last = dve.bn_stats(st[:, n, t, :], src[:, t, :])
                last.then_inc(d_st[n].sem, 1)
                dve.wait_ge(s_zero, 1)
                dve.wait_ge(d_st[n].sem, d_st[n].at(s))
                for t in range(NT):
                    last = dve.bn_aggr(mv[:, n, t, :], st[:, n, t, :])
                last.then_inc(d_mv[n].sem, 1)
                dve.wait_ge(d_mv[n].sem, d_mv[n].at(s))
                ts(vpe[:, n, :], mv[:, n, :, 1], EPS, None, ALU.add).then_inc(d_vpe[n].sem, 1)

            def norm(n, s, src, dst, done):
                dve.wait_ge(g_rstd[n].sem, g_rstd[n].at(s))
                for t in range(NT):
                    last = ts(dst[:, t, :], src[:, t, :], mv[:, n, t, 0:1], rstd[:, n, t:t + 1], ALU.subtract, ALU.mult)
                last.then_inc(done.sem, 1)

            dve.memset(xTs[:, 1], 0.0)
            dve.memset(Sd[:, :, :], 0.0)
            dve.memset(Sn[:, :, :], 0.0)
            dve.memset(mhalf[:, :], -0.5)
            dve.memset(Vs.rearrange("p s t g b f -> p (s t g) b f")[:, :, 1, :], 0.0).then_inc(s_zero, 1)
            dve.wait_ge(s_vec, 16)
            ts(qb[:, :], vec[:, 5, :], SCALE, None, ALU.mult).then_inc(s_qb, 1)
            dve.wait_ge(s_att, 16 * 3)
            ts(flat(Wp[:, WQ]), flat(Wp[:, WQ]), SCALE, None, ALU.mult).then_inc(s_qb, 1)
            wc = wc_raw.rearrange("p w j d -> p w (j d)")
            wh, wl = (Wc[:, :, n].rearrange("p w j d -> p w (j d)") for n in range(2))
            dve.tensor_copy(wh, wc).then_inc(s_wc, 1)
            dve.wait_ge(s_wc, 1)
            tt(wl, wc, wh.bitcast(F32), ALU.subtract).then_inc(s_wc, 1)
            dve.wait_ge(s_const, 16 * 6)
            dve.wait_ge(s_pick, 32)
            dve.tensor_copy(pick.rearrange("p n b f -> p (n b f)"), flat(Sc[:, 0])).then_inc(s_picked, 1)
            dve.tensor_copy(selh.rearrange("p n c -> p (n c)"), Sc[0:2 * HEADS, 1, 0]).then_inc(s_picked, 1)
            dve.tensor_copy(sele[:, :], sele_raw[:, 0:E]).then_inc(s_small, 1)
            ts(minus_low[:, :], sele_raw[:, E:E + 1], -1.0, None, ALU.mult).then_inc(s_small, 1)
            dve.tensor_copy(Wgs[:, 0], Wg[:, :, :]).then_inc(s_small, 1)
            dve.wait_ge(s_small, 3)
            tt(Wgs[:, 1], Wg[:, :, :], Wgs[:, 0].bitcast(F32), ALU.subtract).then_inc(s_small, 1)
            dve.wait_ge(s_decay, 1)

            def a_chunk(s, n):
                if n == 1:
                    dve.wait_ge(p_kvr.sem, p_kvr.at(s, 2))
                    dve.wait_ge(a_ek.sem, a_ek.at(s))
                    if not first(s):
                        dve.wait_ge(g_state.sem, g_state.at(s.plus(-1)))
                    tt(ekv[:, :, :], ek[:, :, :], M, ALU.mult).then_inc(d_ekv.sem, 1)
                elif n == 2:
                    dve.wait_ge(g_den.sem, g_den.at(s))
                    dve.reciprocal(den[:, 0, :], den[:, 0, :]).then_inc(d_rden.sem, 1)
                elif n == 3:
                    dve.wait_ge(a_thr.sem, a_thr.at(s))
                    stt(flat(num[:, :, :]), flat(thr[:, :, :]), 1.0, flat(num[:, :, :]), ALU.add, ALU.mult).then_inc(d_num.sem, 1)
                    dve.reciprocal(den[:, 1, :], den[:, 1, :]).then_inc(d_rden.sem, 1)
                    dve.wait_ge(d_rden.sem, d_rden.at(s))
                    dve.wait_ge(d_num.sem, d_num.at(s))
                    tt(num[:, :, :], num[:, :, :], den[:, :, :], ALU.mult).then_inc(d_wkv.sem, 1)
                elif n == 4:
                    dve.wait_ge(p_v.sem, p_v.at(s))
                    for t in range(NT):
                        bv, v = (r.rearrange("p (g b f) -> p g b f", b=2, f=HD) for r in (bv_row[:, :], M[:, t, :]))
                        last = tt(Vs[:, s.par, t, :, 0:3:2, :], bv, v, ALU.add)
                    last.then_inc(d_v.sem, 1)
                elif n == 5:
                    dve.wait_ge(p_wout.sem, p_wout.at(s))
                    if not first(s):
                        dve.wait_ge(p_x1T.sem, p_x1T.at(s.plus(-1)))
                        dve.wait_ge(g_x1b.sem, g_x1b.at(s.plus(-1)))
                    dve.wait_ge(s_x, 16 * (s.l + 1))
                    stt(x1[:, :, :], M, 0.5, xs[:, :, :], ALU.mult, ALU.add).then_inc(d_z1.sem, 1)
                    dve.wait_ge(d_z1.sem, d_z1.at(s))
                    moments(0, s, x1)
                elif n == 7:
                    dve.wait_ge(a_q.sem, a_q.at(s))
                    for j in range(ND):
                        last = stt(QT[:, 1, j, :], M[:, j, :], qb[:, j:j + 1], QT[:, 0, j, :].bitcast(F32), ALU.add, ALU.subtract)
                    last.then_inc(d_q.sem, 1)
                elif n == 8:
                    dve.wait_ge(a_k.sem, a_k.at(s))
                    for j in range(ND):
                        last = stt(KT[:, 1, j, :], M[:, j, :], vec[:, 6, j:j + 1], KT[:, 0, j, :].bitcast(F32), ALU.add, ALU.subtract)
                    last.then_inc(d_k.sem, 1)

            def clip(s, h, two):
                if first(s) and h == 0:
                    dve.wait_ge(s_picked, 2)
                dve.wait_ge(p_s.sem, p_s.at(s, h + 1))
                if h >= SBUFS:
                    dve.wait_ge(p_t.sem, p_t.at(s, h - SBUFS + 1))
                elif not first(s):
                    dve.wait_ge(p_t.sem, p_t.at(s.plus(-1)))
                ts(flat(Sc[:, h % SBUFS]), (bG if two and h % 2 else bS)[:, :], CLAMP, -CLAMP, ALU.min, ALU.max).then_inc(d_clip.sem, 1)
                dve.wait_ge(d_clip.sem, d_clip.at(s, h + 1))
                dve.tensor_reduce(nmx[:, h, :], Sc[:, h % SBUFS], AX.X, ALU.max, negate=True).then_inc(d_max.sem, 1)

            def low_rows(rows):
                return stt(rows[:, :], rows[:, :].bitcast(F32), minus_low[:, :], bM[0:2 * E, 0:TOK], ALU.mult, ALU.add)

            def t_chunk(s, n):
                if n == 0:
                    dve.wait_ge(a_exp.sem, a_exp.at(s))
                    for n in range(2):
                        last = dve.reciprocal(rr[:, :, n, :], rs[:, s.par])
                    last.then_inc(d_rr.sem, 1)
                elif n == 1:
                    dve.wait_ge(p_R.sem, p_R.at(s))
                    dve.wait_ge(a_o.sem, a_o.at(s))
                    tt(ao[:, :, :], ao[:, :, :], M, ALU.mult).then_inc(d_ao.sem, 1)
                elif n == 2:
                    dve.wait_ge(p_wo.sem, p_wo.at(s))
                    dve.wait_ge(g_x1b.sem, g_x1b.at(s))
                    tt(x2[:, s.par], x1b[:, s.par], M, ALU.add).then_inc(d_z2.sem, 1)
                elif n == 3:
                    dve.wait_ge(a_x2T.sem, a_x2T.at(s))
                    tt(x2T[:, s.par, 1], M, x2T[:, s.par, 0].bitcast(F32), ALU.subtract).then_inc(d_x2T.sem, 1)

            def router(s, part):
                step = [ROUTER_SIGNALS[part]]

                def did(ins):
                    step[0] += 1
                    ins.then_inc(d_gate.sem, 1)
                    return step[0]

                def after(k):
                    dve.wait_ge(d_gate.sem, d_gate.at(s, k))

                v = sc[:, :, :].rearrange("p t (g e) -> p (t g) e", e=EG)

                def ranks(val, gt, eq, rank, n):
                    for t in range(NT):
                        vj = val[:, t, :].rearrange("p (a e) -> p a e", a=1).to_broadcast([P, n, n])
                        vi = val[:, t, :].rearrange("p (e a) -> p e a", a=1).to_broadcast([P, n, n])
                        tt(gt[:, t], vj, vi, ALU.is_gt)
                        last = tt(eq[:, t], vj, vi, ALU.is_equal)
                    k = did(last)
                    after(k)
                    for t in range(NT):
                        last = tt(eq[:, t], eq[:, t], lower[:, 0:n, 0:n], ALU.mult)
                    after(did(last))
                    after(did(tt(gt.rearrange("p t i j -> p (t i j)"), gt.rearrange("p t i j -> p (t i j)"),
                                 eq.rearrange("p t i j -> p (t i j)"), ALU.add)))
                    did(dve.tensor_reduce(rank, gt.rearrange("p t i j -> p (t i) j"), AX.X, ALU.add))

                if part == 0:
                    dve.wait_ge(a_gate.sem, a_gate.at(s))
                    after(did(ts(flat(sc[:, :, :]), gth[:, :], 0.5, 0.5, ALU.mult, ALU.add)))
                    for n, (i, j) in enumerate([(0, 1), (0, 2), (0, 3), (1, 2), (1, 3), (2, 3)]):
                        last = tt(pair[:, :, n:n + 1], v[:, :, i:i + 1], v[:, :, j:j + 1], ALU.add)
                    after(did(last))
                    after(did(dve.tensor_reduce(gsum[:, :, :].rearrange("p t g -> p (t g)"), pair[:, :, :], AX.X, ALU.max)))
                    ranks(gsum, ggt[:, :, :, :], geq[:, :, :, :], grank[:, :, :].rearrange("p t g -> p (t g)"), GROUPS)
                elif part == 1:
                    after(step[0])
                    after(did(ts(gok[:, :, :], grank[:, :, :], float(TOPG) - 0.5, 2.0, ALU.is_lt, ALU.mult)))
                    m4 = msk[:, :, :].rearrange("p t (g e) -> p (t g) e", e=EG)
                    g4 = gok[:, :, :].rearrange("p t (g a) -> p (t g) a", a=1).to_broadcast([P, NT * GROUPS, EG])
                    after(did(tt(m4, v, g4, ALU.mult)))
                    ranks(msk, egt, eeq, erank[:, :, :].rearrange("p t e -> p (t e)"), E)
                else:
                    after(step[0])
                    for t in range(NT):
                        last = stt(wsel[:, t, :], erank[:, t, :], float(TOPK) - 0.5, sc[:, t, :], ALU.is_lt, ALU.mult,
                                   accum_out=wsum[:, t:t + 1])
                    last.then_inc(d_wsel.sem, 1)
                    dve.wait_ge(d_wsel.sem, d_wsel.at(s))
                    ts(wrec[:, :], wsum[:, :], 1e-6, None, ALU.add).then_inc(d_wsum.sem, 1)
                    dve.wait_ge(d_wsum.sem, d_wsum.at(s))
                    dve.reciprocal(wrec[:, :], wrec[:, :]).then_inc(d_wrec.sem, 1)
                    dve.wait_ge(d_wrec.sem, d_wrec.at(s))
                    for t in range(NT):
                        for n in range(2):
                            last = ts(comb[:, t, n, :], wsel[:, t, :], wrec[:, t:t + 1], None, ALU.mult)
                    last.then_inc(d_comb.sem, 1)
                assert step[0] == ROUTER_SIGNALS[part + 1], step[0]

            def hidden_gate(s, k):
                dve.wait_ge(a_tg.sem, a_tg.at(s, k + 1))
                t1 = flat(tg[:, :, :])
                stt(t1, t1, 1.0, bG[:, :], ALU.add, ALU.mult).then_inc(d_t1.sem, 1)

            def hidden_up(s, k):
                dve.wait_ge(d_t1.sem, d_t1.at(s, k + 1))
                dve.wait_ge(p_u.sem, p_u.at(s, k + 1))
                if k >= 2:
                    dve.wait_ge(p_y.sem, p_y.at(s, k - 1))
                elif not first(s):
                    dve.wait_ge(p_y.sem, p_y.at(s.plus(-1)))
                tt(flat(hid[:, k % 2]), flat(tg[:, :, :]), bU[:, :], ALU.mult).then_inc(d_t2.sem, 1)

            def hidden_combine(s, k):
                h = flat(hid[:, k % 2])
                dve.wait_ge(p_c.sem, p_c.at(s, k))
                dve.wait_ge(d_t2.sem, d_t2.at(s, k + 1))
                tt(h, h, bC[:, :], ALU.mult).then_inc(d_t3.sem, 1)

            def last_sum(s):
                dve.wait_ge(p_y.sem, p_y.at(s))
                if not first(s):
                    dve.wait_ge(s_out, 16 * s.l)
                stt(yo[:, :, :], cols(bY), 0.5, x2[:, s.par], ALU.mult, ALU.add).then_inc(d_z3.sem, 1)

            def body(s, A=False, B=False, T=False, C=False, F=False):
                a, t, c, f = s.plus(1), s.plus(-1), s.plus(-2), s.plus(-3)
                for k in range(PAIRS + 1):
                    h = 2 * k
                    heads = B and h < HEADS
                    if heads:
                        clip(s, h, not C)
                    if A and k == 6:
                        norm(0, a, x1, x1, d_x1)
                    if T and k == TAIL_AT[2] + 1:
                        norm(1, t, x2[:, t.par], x2[:, t.par], d_x2)
                    if F and k == 2:
                        norm(2, f, yo[:, :, :], yo[:, :, :], d_yo)
                    if C and k < PAIRS:
                        hidden_gate(c, k)
                        hidden_up(c, k)
                    if C and k == 0:
                        dve.wait_ge(a_comb.sem, a_comb.at(c))
                        low_rows(combT).then_inc(d_combT.sem, 1)
                    if T and k == 0:
                        t_chunk(t, 0)
                    if T and k == TAIL_AT[0]:
                        dve.wait_ge(a_rT.sem, a_rT.at(t))
                        low_rows(rT).then_inc(d_rT.sem, 1)
                    if T and k in TAIL_AT[1:]:
                        t_chunk(t, TAIL_AT.index(k))
                    if heads:
                        clip(s, h + 1, not C)
                    if F and k == 0:
                        last_sum(f)
                    if C and 0 < k < PAIRS:
                        hidden_combine(c, k)
                    if F and k == 1:
                        dve.wait_ge(d_z3.sem, d_z3.at(f))
                        moments(2, f, yo[:, :, :])
                    if T and k == TAIL_AT[2]:
                        dve.wait_ge(d_z2.sem, d_z2.at(t))
                        moments(1, t, x2[:, t.par])
                    if A and k == 8:
                        a_chunk(a, k)
                    if T and k in ROUTER_AT:
                        router(t, ROUTER_AT.index(k))
                    if A and k < 8:
                        a_chunk(a, k)

            bodies(dve, body)

        @block.gpsimd
        def _(pool):
            def rsqrt(n, s):
                pool.wait_ge(d_vpe[n].sem, d_vpe[n].at(s))
                pool.tensor_tensor(rstd[:, n, :], vpe[:, n, :], mhalf[:, :], ALU.pow).then_inc(g_rstd[n].sem, 1)

            def split_experts(until):
                for n in range(SPLIT_BY[SPLIT_BY.index(until) - 1], until):
                    w, c = n // NWCH, n % NWCH * WCH
                    pool.wait_ge(s_raw[n % 2], 16 * (n // 2 + 1))
                    pool.tensor_copy(W13[:, w, 0, :, c:c + WCH], wraw[:, n % 2]).then_inc(s_high, 1)
                    pool.wait_ge(s_high, n + 1)
                    pool.tensor_tensor(W13[:, w, 1, :, c:c + WCH], wraw[:, n % 2], W13[:, w, 0, :, c:c + WCH].bitcast(F32),
                                       ALU.subtract).then_inc(s_split, 1)

            def mixes(s):
                pool.wait_ge(s_xT[s.par], 16 * (s.half + 1))
                now, before = xTs[:, s.par], xTs[:, 1 - s.par]
                if not first(s):
                    pool.wait_ge(p_kvr.sem, p_kvr.at(s.plus(-1)))
                pool.tensor_tensor(dx, now, before, ALU.subtract).then_inc(g_dx.sem, 1)
                pool.wait_ge(g_dx.sem, g_dx.at(s))
                for m in range(3):
                    mu = vec[:, m, :].rearrange("p (j a) -> p j a", a=1).to_broadcast([P, ND, TOK])
                    if m == 2:
                        pool.wait_ge(g_dmix.sem, g_dmix.at(s, 2))
                    pool.tensor_tensor(mix[:, m], dx, mu, ALU.mult).then_inc(g_dmix.sem, 1)
                    pool.wait_ge(g_dmix.sem, g_dmix.at(s, m + 1))
                    pool.tensor_tensor(mix[:, m], mix[:, m], before, ALU.add).then_inc(g_mix.sem, 1)

            def sums(s):
                pool.wait_ge(a_ek.sem, a_ek.at(s))
                pool.wait_ge(d_ekv.sem, d_ekv.at(s))
                by = eu[:, :].rearrange("p (j a) -> p j a", a=1).to_broadcast([P, ND, TOK])
                pool.tensor_tensor(den[:, :, :], ek[:, :, :], by, ALU.mult).then_inc(g_den.sem, 1)
                pool.tensor_tensor(num[:, :, :], ekv[:, :, :], by, ALU.mult).then_inc(g_den.sem, 1)
                pool.wait_ge(g_den.sem, g_den.at(s, 2))
                pool.tensor_tensor(den[:, :, :], den[:, :, :], Sd[:, :, :], ALU.add).then_inc(g_den.sem, 1)
                pool.tensor_tensor(num[:, :, :], num[:, :, :], Sn[:, :, :], ALU.add).then_inc(g_den.sem, 1)
                pool.wait_ge(g_den.sem, g_den.at(s))
                by = decay[:, :].rearrange("p (j a) -> p j a", a=1).to_broadcast([P, ND, TOK])
                pool.tensor_tensor(Sd[:, :, :], Sd[:, :, :], by, ALU.mult).then_inc(g_state.sem, 1)
                pool.tensor_tensor(Sn[:, :, :], Sn[:, :, :], by, ALU.mult).then_inc(g_state.sem, 1)
                pool.wait_ge(g_state.sem, g_state.at(s, 2))
                pool.tensor_tensor(Sd[:, :, :], Sd[:, :, :], ek[:, :, :], ALU.add).then_inc(g_state.sem, 1)
                pool.tensor_tensor(Sn[:, :, :], Sn[:, :, :], ekv[:, :, :], ALU.add).then_inc(g_state.sem, 1)

            def body(s, A=False, B=False, T=False, C=False, F=False, mix_next=True, experts=None):
                a, t, c, f = s.plus(1), s.plus(-1), s.plus(-2), s.plus(-3)
                if F:
                    rsqrt(2, f)
                if A:
                    pool.wait_ge(a_ctx.sem, a_ctx.at(a))
                    pool.tensor_tensor(cTs[:, 1], cT, cTs[:, 0].bitcast(F32), ALU.subtract).then_inc(g_ctx.sem, 1)
                    pool.wait_ge(g_ctx.sem, g_ctx.at(a))
                    sums(a)
                if experts is not None:
                    split_experts(experts)
                if T:
                    rsqrt(1, t)
                if A:
                    rsqrt(0, a)
                    pool.wait_ge(d_x1.sem, d_x1.at(a))
                    if T:
                        pool.wait_ge(d_z2.sem, d_z2.at(t))
                    for n in range(NT):
                        last = pool.tensor_tensor(x1b[:, a.par, n, :], x1[:, n, :], bo_row[:, :], ALU.add)
                    last.then_inc(g_x1b.sem, 1)
                    if mix_next:
                        mixes(a.plus(1))

            pool.wait_ge(s_zero, 1)
            pool.wait_ge(s_vec, 16)
            pool.wait_ge(s_decay, 1)
            mixes(Step(0, 0))
            body(Step(0, -1), A=True)
            split_experts(SPLIT_BY[1])
            body(Step(0, 0), A=True, B=True, experts=SPLIT_BY[2])
            split_experts(SPLIT_BY[3])
            body(Step(0, 1), A=True, B=True, T=True, experts=SPLIT_BY[4])
            split_experts(SPLIT_BY[5])
            body(Step(0, 2), A=True, B=True, T=True, C=True)
            with pool.Fori(1, (L - 4) // 2) as i:
                body(Step(i, 1), A=True, B=True, T=True, C=True, F=True)
                body(Step(i, 2), A=True, B=True, T=True, C=True, F=True)
            body(Step((L - 4) // 2, 1), A=True, B=True, T=True, C=True, F=True)
            body(Step((L - 4) // 2, 2), A=True, B=True, T=True, C=True, F=True, mix_next=False)
            last_bodies(body)


def kernel(**inputs):
    import concourse.bacc as _bacc
    from concourse.bass_utils import run_bass_kernel_spmd as _run

    a = {k: np.asarray(v) for k, v in inputs.items()}
    at, xa, ff = "L0_attn_", "L0_xattn_", "L0_ffn_"

    def column(v):
        return v.reshape(ND, P).T

    p = np.arange(P)
    same = (p[:, None] // HD % 2 == p[None, :] // 64) & (p[:, None] % HD == p[None, :] % HD)
    block = p[None, :] // HD % 4
    picks = np.stack([same & (block % 2 == 0), same & (block % 2 == 1), same & (block < 2), same & (block >= 2)]).astype(np.float32)
    arrays = {
        "x": a["x"],
        "xT": a["x"].transpose(0, 2, 1),
        "ctxT": a["ctx_768"].transpose(0, 2, 1),
        "vecs": np.stack([column(a[at + "mu_k"]), column(a[at + "mu_v"]), column(a[at + "mu_r"]), column(a[at + "w"]),
                          column(a[at + "u"]), column(a[xa + "bq"]), column(a[xa + "bk"])], axis=1),
        "rows": np.stack([np.broadcast_to(a[xa + "bv"], (P, D)), np.broadcast_to(a[xa + "bo"], (P, D))]),
        "wproj": np.stack([a[at + "Wk"].T, a[at + "Wv"].T, a[at + "Wr"].T, a[at + "W_out"].T, a[xa + "Wq"]]),
        "wctx": np.stack([a[xa + "Wk"], a[xa + "Wv"]]),
        "wo": a[xa + "Wo"],
        "w1": np.concatenate([a[ff + "w1_s"], a[ff + "w1_e"].reshape(E * F, D)]).T,
        "w3": np.concatenate([a[ff + "w3_s"], a[ff + "w3_e"].reshape(E * F, D)]).T,
        "w2": np.concatenate([a[ff + "w2_s"].T.reshape(2, P, D), a[ff + "w2_e"].transpose(0, 2, 1)]),
        "wg": a[ff + "w_gate"].T,
        "ident": np.eye(P, dtype=np.float32),
        "sel": (np.arange(2 * HEADS)[:, None, None] % HEADS == HG * np.arange(ND)[None, :, None] + p[None, None, :] // HD).astype(np.float32),
        "sel2": np.concatenate([np.concatenate([np.eye(E), np.zeros((E, 1))], 1), np.concatenate([np.eye(E), np.ones((E, 1))], 1)]).astype(np.float32),
        "picks": picks,
        "below": np.ascontiguousarray(np.broadcast_to(np.tril(np.ones((E, E), np.float32), -1), (P, E, E))),
    }
    nc = _bacc.Bacc("TRN2", target_bir_lowering=False, num_devices=1)
    args = []
    for name, v in arrays.items():
        arrays[name] = v = np.ascontiguousarray(v)
        args.append(nc.dram_tensor(name, v.shape, mybir.dt.from_np(v.dtype), kind="ExternalInput").ap())
    out = nc.dram_tensor("out", (L, TOK, D), F32, kind="ExternalOutput").ap()
    decoder_layer(nc, *args, out)
    return _run(nc, [arrays], core_ids=[0]).results[0]["out"]
```
